# Optimizing a Trainium2 kernel written in Bass

```python
import numpy as np
import jax
import jax.numpy as jnp

def _softmax(x, axis=-1):
    return jax.nn.softmax(x, axis=axis)

def _gelu(x):
    return jax.nn.gelu(x, approximate=True)

def _silu(x):
    return jax.nn.silu(x)

def _sigmoid(x):
    return jax.nn.sigmoid(x)

def _layernorm(x, axis=-1, eps=1e-05):
    m = jnp.mean(x, axis=axis, keepdims=True)
    v = jnp.var(x, axis=axis, keepdims=True)
    return (x - m) / jnp.sqrt(v + eps)

def _scatter_add(tgt, idx, src, axis=0):
    return tgt.at[idx].add(src)

def _segment_sum(src, seg, n):
    return jax.ops.segment_sum(src, seg, n)
kernel_name = 'mk_prb_d1_jaxref_r4_2dd148'

def setup_inputs(seed: int=0):
    np.random.seed(seed)
    _w = jnp.asarray

    def _L0_attn_setup():
        import jax, jax.numpy as jnp
        import numpy as np
        import math
        N_HEAD = 16
        N_EMBD = 256
        HEAD_D = N_EMBD // N_HEAD
        BASE = 2500

        def rope(Y):
            d = Y.shape[-1]
            t = Y.shape[-2]
            theta = BASE ** (-2.0 * jnp.arange(d // 2, dtype=Y.dtype) / d)
            theta2 = jnp.concatenate([theta, theta], axis=0)
            pos = jnp.arange(1, t + 1, dtype=Y.dtype)
            C = pos[:, None] * theta2[None, :]
            cos, sin = (jnp.cos(C), jnp.sin(C))
            Y2 = jnp.concatenate([-Y[..., d // 2:], Y[..., :d // 2]], axis=-1)
            return Y * cos + Y2 * sin
        key = jax.random.key(seed)
        ks = jax.random.split(key, 9)
        s = 0.02
        x = jax.random.normal(ks[0], (4, 512, N_EMBD), dtype=jnp.float32)
        Wq = jax.random.normal(ks[1], (N_EMBD, N_EMBD), dtype=jnp.float32) * s
        bq = jnp.zeros((N_EMBD,), dtype=jnp.float32)
        Wk = jax.random.normal(ks[2], (N_EMBD, N_EMBD), dtype=jnp.float32) * s
        bk = jnp.zeros((N_EMBD,), dtype=jnp.float32)
        Wv = jax.random.normal(ks[3], (N_EMBD, N_EMBD), dtype=jnp.float32) * s
        bv = jnp.zeros((N_EMBD,), dtype=jnp.float32)
        Wo = jax.random.normal(ks[4], (N_EMBD, N_EMBD), dtype=jnp.float32) * s
        bo = jnp.zeros((N_EMBD,), dtype=jnp.float32)
        return {'x': x, 'Wq': Wq, 'bq': bq, 'Wk': Wk, 'bk': bk, 'Wv': Wv, 'bv': bv, 'Wo': Wo, 'bo': bo}
    _L0_attn_in = _L0_attn_setup()

    def _L0_ffn_setup():
        import jax, jax.numpy as jnp
        import numpy as np
        IN_F, OUT_F, BLOCK, NBLK = (256, 1024, 64, 16)
        TOPK = NBLK // 4
        key = jax.random.key(seed)
        ks = jax.random.split(key, 7)
        s = 1.0 / np.sqrt(IN_F)
        s2 = 1.0 / np.sqrt(OUT_F)
        return {'x': jax.random.normal(ks[0], (4, 1024, IN_F), jnp.float32), 'router_w': jax.random.uniform(ks[1], (NBLK, IN_F), jnp.float32, -s, s), 'router_b': jax.random.uniform(ks[2], (NBLK,), jnp.float32, -s, s), 'w1': jax.random.uniform(ks[3], (OUT_F, IN_F), jnp.float32, -s, s), 'b1': jax.random.uniform(ks[4], (OUT_F,), jnp.float32, -s, s), 'w2': jax.random.uniform(ks[5], (IN_F, OUT_F), jnp.float32, -s2, s2), 'b2': jax.random.uniform(ks[6], (IN_F,), jnp.float32, -s2, s2)}
    _L0_ffn_in = _L0_ffn_setup()
    _d = {'L0_attn_x': _L0_attn_in['x'], 'L0_attn_Wq': _L0_attn_in['Wq'], 'L0_attn_bq': _L0_attn_in['bq'], 'L0_attn_Wk': _L0_attn_in['Wk'], 'L0_attn_bk': _L0_attn_in['bk'], 'L0_attn_Wv': _L0_attn_in['Wv'], 'L0_attn_bv': _L0_attn_in['bv'], 'L0_attn_Wo': _L0_attn_in['Wo'], 'L0_attn_bo': _L0_attn_in['bo'], 'L0_ffn_router_w': _L0_ffn_in['router_w'], 'L0_ffn_router_b': _L0_ffn_in['router_b'], 'L0_ffn_w1': _L0_ffn_in['w1'], 'L0_ffn_b1': _L0_ffn_in['b1'], 'L0_ffn_w2': _L0_ffn_in['w2'], 'L0_ffn_b2': _L0_ffn_in['b2']}
    _x0 = _d['L0_attn_x']
    _d['L0_attn_x'] = jax.random.normal(jax.random.fold_in(jax.random.key(seed), 1), (4, 1024, 256), dtype=_x0.dtype)
    del _x0
    return _d

def reference(L0_attn_x, L0_attn_Wq, L0_attn_bq, L0_attn_Wk, L0_attn_bk, L0_attn_Wv, L0_attn_bv, L0_attn_Wo, L0_attn_bo, L0_ffn_router_w, L0_ffn_router_b, L0_ffn_w1, L0_ffn_b1, L0_ffn_w2, L0_ffn_b2):

    def _L0_attn_ref(x, Wq, bq, Wk, bk, Wv, bv, Wo, bo):
        import jax, jax.numpy as jnp
        import numpy as np
        import math
        N_HEAD = 16
        N_EMBD = 256
        HEAD_D = N_EMBD // N_HEAD
        BASE = 2500

        def rope(Y):
            d = Y.shape[-1]
            t = Y.shape[-2]
            theta = BASE ** (-2.0 * jnp.arange(d // 2, dtype=Y.dtype) / d)
            theta2 = jnp.concatenate([theta, theta], axis=0)
            pos = jnp.arange(1, t + 1, dtype=Y.dtype)
            C = pos[:, None] * theta2[None, :]
            cos, sin = (jnp.cos(C), jnp.sin(C))
            Y2 = jnp.concatenate([-Y[..., d // 2:], Y[..., :d // 2]], axis=-1)
            return Y * cos + Y2 * sin
        b, t, _ = x.shape

        def split_heads(y):
            return y.reshape(b, t, N_HEAD, HEAD_D).transpose(0, 2, 1, 3)
        q = split_heads(x @ Wq.T + bq)
        k = split_heads(x @ Wk.T + bk)
        v = split_heads(x @ Wv.T + bv)
        q, k = (rope(q), rope(k))
        scale = math.sqrt(HEAD_D)
        att = jnp.einsum('bhqd,bhkd->bhqk', q, k) / scale
        mask = jnp.tril(jnp.ones((t, t), dtype=bool))
        att = jnp.where(mask, att, -jnp.inf)
        att = jax.nn.softmax(att, axis=-1)
        y = jnp.einsum('bhqk,bhkd->bhqd', att, v)
        y = y.transpose(0, 2, 1, 3).reshape(b, t, N_EMBD)
        return y @ Wo.T + bo

    def _L0_ffn_ref(x, router_w, router_b, w1, b1, w2, b2):
        import jax, jax.numpy as jnp
        import numpy as np
        IN_F, OUT_F, BLOCK, NBLK = (256, 1024, 64, 16)
        TOPK = NBLK // 4
        x_shape = x.shape
        xf = x.reshape(-1, IN_F)
        n = xf.shape[0]
        prob = jax.nn.softmax(xf @ router_w.T + router_b, axis=-1)
        _, idx = jax.lax.top_k(prob, TOPK)
        mask = jnp.zeros((n, NBLK), bool).at[jnp.arange(n)[:, None], idx].set(True)
        w1b = w1.reshape(NBLK, BLOCK, IN_F)
        b1b = b1.reshape(NBLK, BLOCK)
        h = jnp.einsum('nd,ibd->nib', xf, w1b) + b1b
        h = jnp.where(mask[:, :, None], h, jnp.zeros((), h.dtype))
        h = jax.nn.relu(h)
        w2b = w2.reshape(IN_F, NBLK, BLOCK)
        y = jnp.einsum('nib,dib->nd', jnp.where(mask[:, :, None], h, 0.0), w2b) + b2
        return y.reshape(x_shape)
    x = L0_attn_x
    xn = _layernorm(x, axis=-1)
    x = x + _L0_attn_ref(xn, L0_attn_Wq, L0_attn_bq, L0_attn_Wk, L0_attn_bk, L0_attn_Wv, L0_attn_bv, L0_attn_Wo, L0_attn_bo) + _L0_ffn_ref(xn, L0_ffn_router_w, L0_ffn_router_b, L0_ffn_w1, L0_ffn_b1, L0_ffn_w2, L0_ffn_b2)
    return x

_drawn_inputs = setup_inputs


def setup_inputs(seed=0):
    import zlib

    import numpy as np

    out = dict(_drawn_inputs(seed))
    spreads = {'L0_attn_bq': (0.0, 0.8),
     'L0_attn_bk': (0.0, 0.8),
     'L0_attn_bv': (0.0, 0.291),
     'L0_attn_bo': (0.0, 0.1)}
    factors = {'L0_attn_Wq': 8.0,
     'L0_attn_Wk': 8.0,
     'L0_attn_Wv': 6.371,
     'L0_ffn_b1': 8.0,
     'L0_ffn_b2': 3.084}
    for name, (base, spread) in spreads.items():
        noise = np.random.default_rng([zlib.crc32(name.encode()), seed]).standard_normal(out[name].shape)
        drawn = base * np.exp(spread * noise) if base else spread * noise
        out[name] = jnp.asarray(drawn.astype(out[name].dtype))
    for name, factor in factors.items():
        out[name] = (out[name] * factor).astype(out[name].dtype)
    return out
```

```python
from contextlib import ExitStack

import numpy as np

import concourse.bass as bass
from concourse import mybir

F32 = mybir.dt.float32
BF16 = mybir.dt.bfloat16
I32 = mybir.dt.int32
ALU = mybir.AluOpType
ACT = mybir.ActivationFunctionType
AX = mybir.AxisListType

P = 128
B, T, D = 4, 1024, 256
H, HD = 16, 16
F, NBLK, TOPK = 1024, 16, 4
NT = T // P
KB = D // P
FB = F // P
GH = 4
NG = H // GH
HALF = 512
QT = T // NG
VW = 2 * HD
NTERM = 6
NPIECE = 3
KROWS = NTERM * HD
SROWS = KROWS + NPIECE
Q_PIECE = (0, 1, 2, 0, 1, 0)
K_PIECE = (0, 0, 0, 1, 1, 2)
BIG = 1e30
LOWEST = -3e38
EPS = 1e-5
SCALE = 1.0 / float(HD) ** 0.5

UNITS = [(c, j) for c in range(2) for j in range(NT) if j * P < (c + 1) * HALF]
NU = len(UNITS)
MAXU = [(i, c, min(HALF, (i + 1) * P - c * HALF)) for i in range(NT) for c in range(2) if c * HALF < (i + 1) * P]
NMAX = GH * len(MAXU)

S_SLOTS, M_SLOTS, P_SLOTS = 3, 3, 3
LAG = 2

N_S = NT // 2 + 8 + 4 * NG + NG * NU * GH + 4
N_M = NT + 1 + NG * NMAX + NG + 2 * NG + 2 * NG + NT // 2
STACK_INC = 16 * 2 * NTERM
DVE_STEPS = 31
BASE = 1
RSQRT_MAGIC = float(0x5F3759DF)
NEWTON = 4
LN_STEPS = 2 * NT + 3 + 3 * NEWTON


def diagonal(c, j):
    return j * P >= c * HALF


class Ring:

    def __init__(self, slots):
        self.slots, self.n = slots, 0

    def take(self):
        self.n += 1
        return self.n - 1


def block_kernel(nc, x, wqT, bq, wkT, bk, wvT, bv, woT, bo, rwT, rb, w1T, b1, w2T, b2,
                 cos_c, sin_c, ident_c, identb_c, tri_c, sel_c, piece_scratch, max_scratch, out):
    with ExitStack() as ctx:
        def sb(name, shape, dt=F32):
            return ctx.enter_context(nc.sbuf_tensor(name, shape, dt))

        def sem(name):
            return ctx.enter_context(nc.semaphore(name))

        s_bank = ctx.enter_context(nc.psum_tensor("s_bank", [P, S_SLOTS, HALF], F32))
        m_bank = ctx.enter_context(nc.psum_tensor("m_bank", [P, M_SLOTS, HALF], F32))
        o_bank = ctx.enter_context(nc.psum_tensor("o_bank", [P, 2, HALF], F32))

        x_sb = sb("x_sb", [P, NT, D])
        xn = sb("xn", [P, NT, D])
        xnT = sb("xnT", [P, KB, T])
        yT = xnT
        acc = sb("acc", [P, NT, D])
        wq_sb = sb("wq_sb", [P, KB, D])
        wk_sb = sb("wk_sb", [P, KB, D])
        wv_sb = sb("wv_sb", [P, KB, D + NBLK])
        wo_sb = sb("wo_sb", [P, KB, D])
        w1_sb = sb("w1_sb", [P, KB, F])
        w2_sb = sb("w2_sb", [P, FB, D])
        bqk_sb = sb("bqk_sb", [P, 2, KB])
        bv_sb = sb("bv_sb", [P, D + NBLK])
        bo_sb = sb("bo_sb", [P, D])
        b2_sb = sb("b2_sb", [P, D])
        b1_sb = sb("b1_sb", [P, FB])
        cos_sb = sb("cos_sb", [P, T])
        sin_sb = sb("sin_sb", [P, T])
        ident = sb("ident", [P, P])
        identb = sb("identb", [P, P], BF16)
        tri = sb("tri", [P, HALF], BF16)
        tri_k = tri[:, HALF - P:HALF]
        sel = sb("sel", [P, FB, P], BF16)
        pieces = sb("pieces", [P, 4, NPIECE, T], BF16)
        q_st = sb("q_st", [P, 2, GH, T], BF16)
        k_st = sb("k_st", [P, 2, GH, T], BF16)
        v_sb = sb("v_sb", [P, NT, H, VW])
        probs = sb("probs", [P, P_SLOTS, GH, HALF])
        hT = sb("hT", [P, FB, QT])
        oT = sb("oT", [P, T])
        y_sb = sb("y_sb", [P, NT, D])
        unsel = sb("unsel", [P, NT, NBLK], BF16)
        unselT = sb("unselT", [P, T], BF16)
        logits = sb("logits", [P, NT, NBLK + TOPK])
        marked = sb("marked", [P, NT, NBLK + TOPK])
        top8 = sb("top8", [P, NT, 8])
        top4 = sb("top4", [P, NT, 8])
        part_max = sb("part_max", [P, 2, GH, NT, 2])
        row_max = sb("row_max", [P, GH * NT])
        max_rest = sb("max_rest", [P, GH * NT])
        max_pc = sb("max_pc", [P, NPIECE, GH * NT], BF16)
        max_pcT = sb("max_pcT", [NPIECE * GH * NT, P], BF16)
        recip = sb("recip", [P, 2, 4, GH])
        stats = sb("stats", [P, NT, 6])
        mv = sb("mv", [P, NT, 2])
        rstd = sb("rstd", [P, NT])
        var = sb("var", [P, NT])
        guess = sb("guess", [P, NT], I32)
        square = sb("square", [P, NT])

        x_in = sem("x_in")
        const_in = sem("const_in")
        wqk_in, wv_in, w1_in, w2_in, wo_in = (sem(n) for n in ("wqk_in", "wv_in", "w1_in", "w2_in", "wo_in"))
        mask_in = sem("mask_in")
        rope_in = sem("rope_in")
        ones_set = sem("ones_set")
        pad_set = sem("pad_set")
        ln0_step, ln_step = sem("ln0_step"), sem("ln_step")
        xn_ready = sem("xn_ready")
        acc_ready = sem("acc_ready")
        s_fill = sem("s_fill")
        s_out = sem("s_out")
        m_fill = sem("m_fill")
        m_out = sem("m_out")
        dve_step = sem("dve_step")
        turned = sem("turned")
        sin_done = sem("sin_done")
        roped = sem("roped")
        high_done = sem("high_done")
        rest_done = sem("rest_done")
        mid_done = sem("mid_done")
        low_done = sem("low_done")
        pieces_out = [sem("pieces_out0"), sem("pieces_out1")]
        stacked = [sem("stacked0"), sem("stacked1")]
        unsel_ready = sem("unsel_ready")
        max_pcs = sem("max_pcs")
        max_out = sem("max_out")
        max_rows = sem("max_rows")
        pv_done = sem("pv_done")
        o_out = sem("o_out")
        stored = sem("stored")

        x_rows = x.rearrange("(b t p) d -> b p t d", p=P, t=NT)
        out_rows = out.rearrange("(b t p) d -> b p t d", p=P, t=NT)
        scratch_out = max_scratch.rearrange("k (r n) -> (k r) n", n=P)

        def quarter(g):
            return slice(g * QT, (g + 1) * QT)

        def rope_pair(r):
            return probs[:, r % 2, 0:2, :], probs[:, r % 2, 2:4, :]

        block = ctx.enter_context(nc.Block())

        @block.sync
        def _(sp):
            for count in (stored, max_out, *pieces_out, *stacked):
                sp.sem_inc(count, BASE)
            sp.dma_start(x_sb[:], x_rows[0]).then_inc(x_in, 16)
            sp.dma_start(ident[:], ident_c).then_inc(const_in, 16)
            sp.dma_start(identb[:], identb_c).then_inc(const_in, 16)
            sp.dma_start(bqk_sb[:, 0, :], bq).then_inc(const_in, 16)
            sp.dma_start(bqk_sb[:, 1, :], bk).then_inc(const_in, 16)
            sp.dma_start(bv_sb[:, 0:D], bv.partition_broadcast(P)).then_inc(const_in, 16)
            sp.dma_start(bv_sb[:, D:D + NBLK], rb.partition_broadcast(P)).then_inc(const_in, 16)
            sp.dma_start(bo_sb[:], bo.partition_broadcast(P)).then_inc(const_in, 16)
            sp.dma_start(b2_sb[:], b2.partition_broadcast(P)).then_inc(const_in, 16)
            sp.dma_start(b1_sb[:], b1).then_inc(const_in, 16)
            sp.dma_start(wq_sb[:], wqT.rearrange("(k p) n -> p k n", p=P)).then_inc(wqk_in, 16)
            sp.dma_start(wk_sb[:], wkT.rearrange("(k p) n -> p k n", p=P)).then_inc(wqk_in, 16)
            sp.dma_start(cos_sb[:], cos_c).then_inc(rope_in, 16)
            sp.dma_start(sin_sb[:], sin_c).then_inc(rope_in, 16)
            sp.dma_start(wv_sb[:, :, 0:D], wvT.rearrange("(k p) n -> p k n", p=P)).then_inc(wv_in, 16)
            sp.dma_start(wv_sb[:, :, D:D + NBLK], rwT.rearrange("(k p) n -> p k n", p=P)).then_inc(wv_in, 16)
            sp.dma_start(sel[:], sel_c).then_inc(mask_in, 16)
            sp.dma_start(tri[:], tri_c).then_inc(mask_in, 16)
            sp.dma_start(w1_sb[:], w1T.rearrange("(k p) n -> p k n", p=P)).then_inc(w1_in, 16)
            sp.dma_start(w2_sb[:], w2T.rearrange("(k p) n -> p k n", p=P)).then_inc(w2_in, 16)
            sp.dma_start(wo_sb[:], woT.rearrange("(k p) n -> p k n", p=P)).then_inc(wo_in, 16)

            def store_pieces(b, r):
                sp.wait_ge(low_done, b * 4 + r + 1)
                if r == 0:
                    for stack in stacked:
                        sp.nop(nofuse=True)
                        sp.wait_ge(stack, b * 2 * STACK_INC + BASE)
                sp.dma_start(piece_scratch[r], pieces[:, r, :, :]).then_inc(pieces_out[r // 2], 16)

            def load_stacks(b, g):
                mb = g // 2
                sp.wait_ge(pieces_out[mb], b * 32 + 32 + BASE)
                sp.nop(nofuse=True)
                sp.wait_ge(pv_done, (b * NG + max(g - 1, 0)) * NU + BASE)
                for qk, stack, order in ((0, q_st, Q_PIECE), (1, k_st, K_PIECE)):
                    heads = piece_scratch[2 * mb + qk, (g % 2) * GH * HD:(g % 2 + 1) * GH * HD]
                    heads = heads.rearrange("(c d) k n -> k d c n", d=HD)
                    for t in range(NTERM):
                        sp.dma_start(stack[t * HD:(t + 1) * HD, g % 2, :, :],
                                     heads[order[t]]).then_inc(stacked[g % 2], 16)

            def place_maxima(b, g):
                sp.wait_ge(m_out, b * N_M + MAX_COPIED[g] + BASE)
                sp.dma_start(scratch_out, max_pcT[:]).then_inc(max_out, 16)
                sp.wait_ge(max_out, (b * NG + g + 1) * 16 + BASE)
                sp.nop(nofuse=True)
                sp.wait_ge(pv_done, (b * NG + max(g - 1, 0)) * NU + BASE)
                sp.dma_start(q_st[KROWS:SROWS, g % 2, :, :],
                             max_scratch.rearrange("k (c n) -> k c n", c=GH)).then_inc(max_rows, 16)

            with sp.Fori(0, B) as b:
                store_pieces(b, 0)
                store_pieces(b, 1)
                load_stacks(b, 0)
                load_stacks(b, 1)
                sp.wait_ge(acc_ready, b + 1)
                sp.nop(nofuse=True)
                sp.dma_start(x_sb[:], x_rows[(b + 1) % B]).then_inc(x_in, 16)
                store_pieces(b, 2)
                store_pieces(b, 3)
                place_maxima(b, 0)
                load_stacks(b, 2)
                place_maxima(b, 1)
                load_stacks(b, 3)
                place_maxima(b, 2)
                place_maxima(b, 3)
                for h in range(2):
                    sp.wait_ge(m_out, b * N_M + N_M - 2 + 2 * h + BASE)
                    sp.nop(nofuse=True)
                    t = slice(h * NT // 2, (h + 1) * NT // 2)
                    sp.dma_start(out_rows[b, :, t, :], acc[:, t, :]).then_inc(stored, 16)
            sp.wait_ge(stored, B * 32 + BASE)
            sp.wait_ge(x_in, 16 * (B + 1))

        @block.gpsimd
        def _(pool):
            nc.gpsimd.memset(v_sb[:, :, :, HD:VW], 1.0).then_inc(ones_set, 1)
            pool.wait_ge(ones_set, 1)
            nc.gpsimd.memset(k_st[KROWS:P, :, :, :], 1.0).then_inc(ones_set, 1)
            pool.wait_ge(ones_set, 2)
            nc.gpsimd.memset(unselT[:], 0.0).then_inc(ones_set, 1)
            pool.wait_ge(const_in, 16 * 9)
            nc.gpsimd.tensor_tensor(bo_sb[:], bo_sb[:], b2_sb[:], ALU.add).then_inc(ones_set, 1)

            with pool.Fori(0, B) as b:
                pool.wait_ge(ones_set, 4)
                pool.wait_ge(x_in, b * 16 + 16)
                pool.wait_ge(stored, b * 32 + BASE)
                nc.gpsimd.tensor_tensor(acc[:], x_sb[:], bo_sb[:, None, :].broadcast_to([P, NT, D]),
                                        ALU.add).then_inc(acc_ready, 1)

                def rope_sin(r):
                    pool.wait_ge(turned, b * 4 + r + 1)
                    if r == 0:
                        pool.wait_ge(rope_in, 32)
                    _, y2 = rope_pair(r)
                    nc.gpsimd.tensor_tensor(y2, y2, sin_sb[:].rearrange("p (c n) -> p c n", c=2),
                                            ALU.mult).then_inc(sin_done, 1)

                def low_piece(r):
                    pool.wait_ge(mid_done, b * 4 + r + 1)
                    _, y2 = rope_pair(r)
                    nc.gpsimd.tensor_tensor(pieces[:, r, 2, :].rearrange("p (c n) -> p c n", c=2), y2,
                                            pieces[:, r, 1, :].rearrange("p (c n) -> p c n", c=2),
                                            ALU.subtract).then_inc(low_done, 1)

                rope_sin(0)
                rope_sin(1)
                low_piece(0)
                low_piece(1)
                rope_sin(2)
                rope_sin(3)
                low_piece(2)
                low_piece(3)

        @block.scalar
        def _(act):
            act.sem_inc(s_out, BASE)
            act.sem_inc(o_out, BASE)
            with act.Fori(0, B) as b:
                ring = Ring(S_SLOTS)

                def filled():
                    n = ring.take()
                    act.wait_ge(s_fill, b * N_S + n + 1)
                    return s_bank[:, n % S_SLOTS, :]

                for t in range(0, NT, 2):
                    bank = filled()
                    if t == 0:
                        act.wait_ge(m_fill, b * N_M + BASE)
                    nc.scalar.activation(xnT[:, :, t * P:(t + 2) * P], bank.rearrange("p (k n) -> p k n", k=KB),
                                         ACT.Copy).then_inc(s_out, 1)

                def project(r):
                    mb, qk = r // 2, r % 2
                    y, _ = rope_pair(r)
                    act.wait_ge(const_in, 16 * 9)
                    if r >= 2:
                        act.wait_ge(low_done, b * 4 + r - 1)
                    else:
                        act.wait_ge(pv_done, b * NG * NU + BASE)
                    for c in range(2):
                        nc.scalar.activation(y[:, c, :], filled(), ACT.Identity,
                                             bias=bqk_sb[:, qk, mb:mb + 1]).then_inc(s_out, 1)

                def high_piece(r):
                    y, _ = rope_pair(r)
                    act.wait_ge(roped, b * 4 + r + 1)
                    if r == 0:
                        for piece_set in pieces_out:
                            act.wait_ge(piece_set, b * 32 + BASE)
                    nc.scalar.activation(pieces[:, r, 0, :].rearrange("p (c n) -> p c n", c=2), y,
                                         ACT.Copy).then_inc(high_done, 1)

                def mid_piece(r):
                    _, y2 = rope_pair(r)
                    act.wait_ge(rest_done, b * 4 + r + 1)
                    nc.scalar.activation(pieces[:, r, 1, :].rearrange("p (c n) -> p c n", c=2), y2,
                                         ACT.Copy).then_inc(mid_done, 1)

                def hidden(q):
                    if q:
                        act.wait_ge(m_fill, b * N_M + ffn2_end[q - 1] + BASE)
                    for u in range(FB // 2):
                        bank = filled()
                        for i in range(2):
                            m = 2 * u + i
                            last = nc.scalar.activation(hT[:, m, :], bank[:, i * QT:(i + 1) * QT], ACT.Relu,
                                                        bias=b1_sb[:, m:m + 1])
                        last.then_inc(s_out, 1)

                def take_o(g, c):
                    act.wait_ge(pv_done, b * NG * NU + g * NU + (4 if c == 0 else NU) + BASE)
                    nc.scalar.activation(oT[:, c * HALF:(c + 1) * HALF], o_bank[:, c, :],
                                         ACT.Copy).then_inc(o_out, 1)

                def exps(g):
                    for k, (c, j) in enumerate(UNITS):
                        n = g * NU + k
                        w = (c + 1) * HALF - max(c * HALF, j * P)
                        act.wait_ge(pv_done, b * NG * NU + max(n - P_SLOTS + 1, 0) + BASE)
                        if n == 0:
                            act.wait_ge(low_done, b * 4 + 4)
                        for h in range(GH):
                            nc.scalar.activation(probs[:, k % P_SLOTS, h, 0:w], filled()[:, 0:w], ACT.Exp,
                                                 scale=SCALE).then_inc(s_out, 1)
                        if k == 6:
                            take_o(g, 0)

                project(0)
                project(1)
                high_piece(0)
                mid_piece(0)
                high_piece(1)
                mid_piece(1)
                hidden(0)
                project(2)
                project(3)
                high_piece(2)
                mid_piece(2)
                high_piece(3)
                mid_piece(3)
                hidden(1)
                for g in range(NG):
                    if g == 1:
                        hidden(2)
                    if g == 3:
                        hidden(3)
                    exps(g)
                    take_o(g, 1)
                for u in range(4):
                    kb, h = u // 2, u % 2
                    nc.scalar.activation(yT[:, kb, h * HALF:(h + 1) * HALF], filled(), ACT.Copy).then_inc(s_out, 1)
                assert ring.n == N_S

        @block.tensor
        def _(pe):
            pe.sem_inc(m_fill, BASE)
            pe.sem_inc(pv_done, BASE)
            with pe.Fori(0, B) as b:
                sring, mring = Ring(S_SLOTS), Ring(M_SLOTS)

                def s_slot():
                    n = sring.take()
                    pe.wait_ge(s_out, b * N_S + max(n - S_SLOTS + 1, 0) + BASE)
                    return s_bank[:, n % S_SLOTS, :]

                def m_slot():
                    n = mring.take()
                    pe.wait_ge(m_out, b * N_M + max(n - M_SLOTS + 1, 0) + BASE)
                    return m_bank[:, n % M_SLOTS, :]

                pe.wait_ge(const_in, 16 * 9)
                pe.wait_ge(xn_ready, b + 1)
                for t in range(0, NT, 2):
                    bank = s_slot()
                    for k in range(KB):
                        for i in range(2):
                            at = k * 2 * P + i * P
                            last = nc.tensor.transpose(bank[:, at:at + P], xn[:, t + i, k * P:(k + 1) * P], ident[:])
                    last.then_inc(s_fill, 1)

                def project(r, c):
                    mb, w = r // 2, (wq_sb, wk_sb)[r % 2]
                    bank = s_slot()
                    for k in range(KB):
                        last = nc.tensor.matmul(bank, w[:, k, mb * P:(mb + 1) * P],
                                                xnT[:, k, c * HALF:(c + 1) * HALF], start=(k == 0), stop=(k == KB - 1))
                    last.then_inc(s_fill, 1)

                pe.wait_ge(s_out, b * N_S + NT // 2 + BASE)
                pe.wait_ge(wqk_in, 32)
                for r in range(2):
                    for c in range(2):
                        project(r, c)

                pe.wait_ge(wv_in, 32)
                for t in range(NT):
                    bank = m_slot()
                    for k in range(KB):
                        last = nc.tensor.matmul(bank[:, 0:D + NBLK], xnT[:, k, t * P:(t + 1) * P], wv_sb[:, k, :],
                                                start=(k == 0), stop=(k == KB - 1))
                    last.then_inc(m_fill, 1)

                bank = m_slot().bitcast(BF16)
                pe.wait_ge(unsel_ready, b + 1)
                for t in range(NT):
                    last = nc.tensor.transpose(bank[0:NBLK, t * P:(t + 1) * P], unsel[:, t, :], identb[:])
                last.then_inc(m_fill, 1)

                def hidden_unit(q, u):
                    bank = s_slot()
                    for i in range(2):
                        m = 2 * u + i
                        o = bank[:, i * QT:(i + 1) * QT]
                        nc.tensor.matmul(o, sel[:, m, :], unselT[:, quarter(q)], start=True, stop=False)
                        for k in range(KB):
                            last = nc.tensor.matmul(o, w1_sb[:, k, m * P:(m + 1) * P], xnT[:, k, quarter(q)],
                                                    start=False, stop=(k == KB - 1))
                    last.then_inc(s_fill, 1)

                def ffn2_part(bank, q, i, k0, k1):
                    for k in range(k0, k1):
                        last = nc.tensor.matmul(bank[:, 0:D], hT[:, k, i * P:(i + 1) * P], w2_sb[:, k, :],
                                                start=(k == 0), stop=(k == FB - 1))
                    if k1 == FB:
                        last.then_inc(m_fill, 1)

                def max_units(g, first, last_):
                    if first == 0:
                        pe.wait_ge(stacked[g % 2], (b * 2 + g // 2 + 1) * STACK_INC + BASE)
                    for n in range(first, last_):
                        h, (i, c, w) = n % GH, MAXU[n // GH]
                        bank = m_slot()
                        nc.tensor.matmul(bank[:, 0:w], q_st[0:KROWS, g % 2, h, i * P:(i + 1) * P],
                                         k_st[0:KROWS, g % 2, h, c * HALF:c * HALF + w],
                                         start=True, stop=True).then_inc(m_fill, 1)

                def turn_maxima(bank, g):
                    pe.wait_ge(max_pcs, b * NG + g + 1)
                    nc.tensor.transpose(bank.bitcast(BF16)[0:NPIECE * GH * NT, 0:P],
                                        max_pc[:].rearrange("p k r -> p (k r)"), identb[:]).then_inc(m_fill, 1)

                def turn_o(g, c):
                    pe.wait_ge(o_out, b * 2 * NG + 2 * g + c + 1 + BASE)
                    bank = m_slot()
                    for t in range(4):
                        last = nc.tensor.transpose(bank[:, t * P:(t + 1) * P],
                                                   oT[:, c * HALF + t * P:c * HALF + (t + 1) * P], ident[:])
                    last.then_inc(m_fill, 1)

                def pv(g, k, out_):
                    c, j = UNITS[k]
                    q0 = max(c * HALF, j * P) - c * HALF
                    pe.wait_ge(s_out, b * N_S + out_ + BASE)
                    if j == 0:
                        pe.wait_ge(o_out, b * 2 * NG + max(2 * g - 1 + c, 0) + BASE)
                    for h in range(GH):
                        last = nc.tensor.matmul(o_bank[h * VW:(h + 1) * VW, c, q0:HALF], v_sb[:, j, g * GH + h, :],
                                                probs[:, k % P_SLOTS, h, 0:HALF - q0], start=(j == 0),
                                                stop=(j == 4 * c + 3), tile_position=(0, h * VW))
                    last.then_inc(pv_done, 1)

                def attend(g):
                    pe.wait_ge(max_rows, (b * NG + g + 1) * 16)
                    base = sring.n
                    for k, (c, j) in enumerate(UNITS):
                        q0 = max(c * HALF, j * P)
                        w = (c + 1) * HALF - q0
                        for h in range(GH):
                            bank = s_slot()
                            last = nc.tensor.matmul(bank[:, 0:w], k_st[0:SROWS, g % 2, h, j * P:(j + 1) * P],
                                                    q_st[0:SROWS, g % 2, h, q0:q0 + w], start=True,
                                                    stop=not diagonal(c, j))
                            if diagonal(c, j):
                                last = nc.tensor.matmul(bank[:, 0:P], tri_k, identb[:], start=False, stop=True)
                            last.then_inc(s_fill, 1)
                            if g + 1 < NG:
                                max_units(g + 1, k * GH + h, k * GH + h + 1)
                        if k == 3 and g:
                            turn_o(g - 1, 0)
                            turn_o(g - 1, 1)
                        if k >= LAG:
                            pv(g, k - LAG, base + (k - LAG + 1) * GH)
                    for k in range(NU - LAG, NU):
                        pv(g, k, base + (k + 1) * GH)

                pe.wait_ge(w1_in, 16)
                pe.wait_ge(mask_in, 32)
                pe.wait_ge(ones_set, 3)
                pe.wait_ge(m_out, b * N_M + NT + 1 + BASE)
                for u in range(4):
                    hidden_unit(0, u)
                n = 0
                for r in range(2, 4):
                    for c in range(2):
                        project(r, c)
                        max_units(0, n, n + 5)
                        n += 5
                pe.wait_ge(w2_in, 16)
                pe.wait_ge(s_out, b * N_S + HIDDEN_DONE[0] + BASE)
                for i in range(2):
                    ffn2_part(m_slot(), 0, i, 0, FB)
                    max_units(0, n, n + 6)
                    n += 6
                for u in range(4):
                    hidden_unit(1, u)
                    max_units(0, n, n + 4)
                    n += 4
                assert n == NMAX

                for g in range(NG):
                    if g in (0, 2):
                        pe.wait_ge(s_out, b * N_S + HIDDEN_DONE[g // 2 + 1] + BASE)
                        turn_bank, tile0 = m_slot(), m_slot()
                        ffn2_part(tile0, g // 2 + 1, 0, 0, 4)
                        turn_maxima(turn_bank, g)
                        ffn2_part(tile0, g // 2 + 1, 0, 4, FB)
                        ffn2_part(m_slot(), g // 2 + 1, 1, 0, FB)
                    else:
                        q = 2 if g == 1 else 3
                        hidden_unit(q, 0)
                        hidden_unit(q, 1)
                        turn_maxima(m_slot(), g)
                        hidden_unit(q, 2)
                        hidden_unit(q, 3)
                    attend(g)

                pe.wait_ge(s_out, b * N_S + HIDDEN_DONE[3] + BASE)
                ffn2_part(m_slot(), 3, 0, 0, FB)
                ffn2_part(m_slot(), 3, 1, 0, FB)
                turn_o(3, 0)
                turn_o(3, 1)
                pe.wait_ge(m_out, b * N_M + N_M - NT // 2 + BASE)
                for u in range(4):
                    kb, h = u // 2, u % 2
                    bank = s_slot()
                    for t in range(4):
                        last = nc.tensor.transpose(bank[:, t * P:(t + 1) * P],
                                                   y_sb[:, 4 * h + t, kb * P:(kb + 1) * P], ident[:])
                    last.then_inc(s_fill, 1)
                pe.wait_ge(wo_in, 16)
                pe.wait_ge(s_out, b * N_S + N_S + BASE)
                for u in range(NT // 2):
                    bank = m_slot()
                    for i in range(2):
                        t = 2 * u + i
                        for k in range(KB):
                            last = nc.tensor.matmul(bank[:, i * D:(i + 1) * D], yT[:, k, t * P:(t + 1) * P],
                                                    wo_sb[:, k, :], start=(k == 0), stop=(k == KB - 1))
                    last.then_inc(m_fill, 1)
                assert sring.n == N_S and mring.n == N_M, (sring.n, mring.n)

        @block.vector
        def _(dve):
            dve.sem_inc(m_out, BASE)
            def plain():
                dve.nop(nofuse=True)

            def layer_norm(rows, step, base):
                dve.wait_ge(x_in, rows * 16 + 16)
                for t in range(NT):
                    nc.vector.bn_stats(stats[:, t, :], x_sb[:, t, :]).then_inc(step, 1)
                dve.wait_ge(step, base + NT)
                plain()
                for t in range(NT):
                    nc.vector.bn_aggr(mv[:, t, :], stats[:, t, :]).then_inc(step, 1)
                dve.wait_ge(step, base + 2 * NT)
                done = base + 2 * NT

                def next_step(ins):
                    nonlocal done
                    ins.then_inc(step, 1)
                    done = done + 1
                    dve.wait_ge(step, done)

                next_step(nc.vector.tensor_scalar(var[:], mv[:, :, 1], EPS, None, ALU.add))
                next_step(nc.vector.tensor_scalar(guess[:], var[:].bitcast(I32), 1, None, ALU.logical_shift_right))
                next_step(nc.vector.tensor_scalar(rstd[:].bitcast(I32), guess[:], -1.0, RSQRT_MAGIC,
                                                  ALU.mult, ALU.add))
                for _ in range(NEWTON):
                    next_step(nc.vector.tensor_tensor(square[:], rstd[:], rstd[:], ALU.mult))
                    next_step(nc.vector.scalar_tensor_tensor(square[:], square[:], -0.5, var[:],
                                                             ALU.mult, ALU.mult))
                    next_step(nc.vector.scalar_tensor_tensor(rstd[:], square[:], 1.5, rstd[:],
                                                             ALU.add, ALU.mult))
                for t in range(NT):
                    last = nc.vector.tensor_scalar(xn[:, t, :], x_sb[:, t, :], mv[:, t, 0:1], rstd[:, t:t + 1],
                                                   ALU.subtract, ALU.mult)
                last.then_inc(xn_ready, 1)

            nc.vector.memset(part_max[:], LOWEST).then_inc(pad_set, 1)
            nc.vector.memset(logits[:], LOWEST).then_inc(pad_set, 1)
            nc.vector.memset(top4[:], LOWEST).then_inc(pad_set, 1)
            layer_norm(0, ln0_step, 0)
            dve.wait_ge(const_in, 16 * 9)
            dve.wait_ge(pad_set, 3)

            with dve.Fori(0, B) as b:
                ring = Ring(M_SLOTS)
                steps = [0]

                def filled():
                    n = ring.take()
                    dve.wait_ge(m_fill, b * N_M + n + 1 + BASE)
                    return m_bank[:, n % M_SLOTS, :]

                def link(ins):
                    steps[0] += 1
                    ins.then_inc(dve_step, 1)
                    dve.wait_ge(dve_step, b * DVE_STEPS + steps[0])

                def turn_halves(r):
                    y, y2 = rope_pair(r)
                    dve.wait_ge(s_out, b * N_S + (8, 16)[r // 2] - 4 + 2 * (r % 2) + 2 + BASE)
                    plain()
                    nc.vector.stream_shuffle(y2, y, [p ^ (HD // 2) for p in range(32)]).then_inc(turned, 1)

                def rope_sum(r):
                    y, y2 = rope_pair(r)
                    if r == 0:
                        dve.wait_ge(rope_in, 32)
                    dve.wait_ge(turned, b * 4 + r + 1)
                    link(nc.vector.tensor_tensor(y, y, cos_sb[:].rearrange("p (c n) -> p c n", c=2), ALU.mult))
                    dve.wait_ge(sin_done, b * 4 + r + 1)
                    nc.vector.tensor_tensor(y, y, y2, ALU.add).then_inc(roped, 1)

                def rest(r):
                    y, y2 = rope_pair(r)
                    dve.wait_ge(high_done, b * 4 + r + 1)
                    nc.vector.tensor_tensor(y2, y, pieces[:, r, 0, :].rearrange("p (c n) -> p c n", c=2),
                                            ALU.subtract).then_inc(rest_done, 1)

                def values(t):
                    bank = filled()
                    if t == 0:
                        dve.wait_ge(pv_done, b * NG * NU + BASE)
                    nc.vector.tensor_tensor(v_sb[:, t, :, 0:HD], bank[:, 0:D].rearrange("p (h d) -> p h d", h=H),
                                            bv_sb[:, 0:D].rearrange("p (h d) -> p h d", h=H), ALU.add)
                    nc.vector.tensor_tensor(logits[:, t, 0:NBLK], bank[:, D:D + NBLK], bv_sb[:, D:D + NBLK],
                                            ALU.add).then_inc(m_out, 1)

                def route():
                    dve.wait_ge(m_out, b * N_M + NT + BASE)
                    plain()
                    for t in range(NT):
                        last = nc.vector.max(top8[:, t, :], logits[:, t, 0:NBLK])
                    link(last)
                    link(nc.vector.tensor_copy(top4[:, :, 0:TOPK], top8[:, :, 0:TOPK]))
                    plain()
                    for t in range(NT):
                        last = nc.vector.match_replace(marked[:, t, :], top4[:, t, :], logits[:, t, :], -LOWEST)
                    link(last)
                    nc.vector.tensor_tensor(unsel[:], marked[:, :, 0:NBLK], logits[:, :, 0:NBLK],
                                            ALU.is_equal).then_inc(unsel_ready, 1)
                    bank = filled().bitcast(BF16)
                    dve.wait_ge(ones_set, 3)
                    nc.vector.tensor_copy(unselT[0:NBLK, :], bank[0:NBLK, :]).then_inc(m_out, 1)

                def max_units(g, first, last_):
                    for n in range(first, last_):
                        h, (i, c, w) = n % GH, MAXU[n // GH]
                        bank = filled()
                        to = part_max[:, g % 2, h, i, c:c + 1]
                        if c * HALF + w == (i + 1) * P:
                            plain()
                            ins = nc.vector.tensor_tensor_reduce(bank[:, 0:w], bank[:, 0:w], tri[:, HALF - w:HALF],
                                                                 1.0, LOWEST, ALU.add, ALU.max, to)
                        else:
                            ins = nc.vector.tensor_reduce(to, bank[:, 0:w], AX.X, ALU.max)
                        ins.then_inc(m_out, 1)

                def split_maxima(g):
                    dve.wait_ge(m_out, b * N_M + ring.n + BASE)
                    link(nc.vector.tensor_reduce(row_max[:], part_max[:, g % 2].rearrange("p h i c -> p (h i) c"),
                                                 AX.X, ALU.max))
                    link(nc.vector.tensor_scalar(max_pc[:, 0, :], row_max[:], -1.0, None, ALU.mult))
                    link(nc.vector.scalar_tensor_tensor(max_rest[:], row_max[:], -1.0, max_pc[:, 0, :],
                                                        ALU.mult, ALU.subtract))
                    link(nc.vector.tensor_copy(max_pc[:, 1, :], max_rest[:]))
                    nc.vector.tensor_tensor(max_pc[:, 2, :], max_rest[:], max_pc[:, 1, :],
                                            ALU.subtract).then_inc(max_pcs, 1)

                def copy_maxima(g):
                    bank = filled()
                    dve.wait_ge(max_out, (b * NG + g) * 16 + BASE)
                    nc.vector.tensor_copy(max_pcT[:], bank.bitcast(BF16)[0:NPIECE * GH * NT, 0:P])\
                        .then_inc(m_out, 1)

                def add_ffn(q, i):
                    bank = filled()
                    t = 2 * q + i
                    dve.wait_ge(acc_ready, b + 1)
                    nc.vector.tensor_tensor(acc[:, t, :], acc[:, t, :], bank[:, 0:D], ALU.add).then_inc(m_out, 1)

                def normalise(g, c):
                    bank = filled().rearrange("p (t h v) -> p t h v", t=4, h=GH)
                    link(nc.vector.reciprocal(recip[:, c], bank[:, :, :, HD]))
                    o = y_sb[:, 4 * c:4 * c + 4, g * GH * HD:(g + 1) * GH * HD].rearrange("p t (h d) -> p t h d", h=GH)
                    nc.vector.tensor_tensor(o, bank[:, :, :, 0:HD],
                                            recip[:, c, :, :, None].broadcast_to([P, 4, GH, HD]),
                                            ALU.mult).then_inc(m_out, 1)

                turn_halves(0)
                rope_sum(0)
                turn_halves(1)
                rope_sum(1)
                values(0)
                rest(0)
                values(1)
                values(2)
                rest(1)
                for t in range(3, NT):
                    values(t)
                route()
                max_units(0, 0, 20)
                turn_halves(2)
                rope_sum(2)
                add_ffn(0, 0)
                turn_halves(3)
                rope_sum(3)
                max_units(0, 20, 22)
                rest(2)
                max_units(0, 22, 26)
                rest(3)
                add_ffn(0, 1)
                max_units(0, 26, NMAX)
                for g in range(NG):
                    split_maxima(g)
                    copy_maxima(g)
                    if g in (0, 2):
                        add_ffn(g // 2 + 1, 0)
                        add_ffn(g // 2 + 1, 1)
                    for k in range(NU):
                        if g + 1 < NG:
                            max_units(g + 1, k * GH, (k + 1) * GH)
                        if k == 3 and g:
                            normalise(g - 1, 0)
                            normalise(g - 1, 1)
                    if g == 3:
                        dve.wait_ge(s_fill, b * N_S + NT // 2)
                        layer_norm(b + 1, ln_step, b * LN_STEPS)
                add_ffn(3, 0)
                add_ffn(3, 1)
                normalise(3, 0)
                normalise(3, 1)
                for u in range(NT // 2):
                    bank = filled()
                    dve.wait_ge(m_out, b * N_M + ring.n - 1 + BASE)
                    nc.vector.tensor_tensor(acc[:, 2 * u:2 * u + 2, :], acc[:, 2 * u:2 * u + 2, :],
                                            bank.rearrange("p (i n) -> p i n", i=2), ALU.add).then_inc(m_out, 1)
                assert ring.n == N_M and steps[0] == DVE_STEPS, (ring.n, steps[0])


ffn2_end = [NT + 1 + 20 + 2 + 6, NT + 1 + NMAX + 2 + 3]
ffn2_end.append(ffn2_end[1] + NMAX + 1 + NMAX + 2 + 3)


HIDDEN_DONE = [12, 20, 20 + NU * GH + 4, 20 + 3 * NU * GH + 8]
MAX_COPIED = [NT + 1 + NMAX + 3]
for _g in range(1, NG):
    MAX_COPIED.append(MAX_COPIED[-1] + (2 if _g in (1, 3) else 0) + NMAX + (2 if _g > 1 else 0) + 1)


def constants():
    theta = np.power(np.float32(2500), (np.float32(-2.0) * np.arange(HD // 2, dtype=np.float32) / np.float32(HD)),
                     dtype=np.float32)
    angle = (np.arange(1, T + 1, dtype=np.float32)[:, None] * theta[None, :]).astype(np.float64)
    lane = np.arange(P) % (HD // 2)
    sign = np.where(np.arange(P) % HD < HD // 2, -1.0, 1.0)
    cos = np.cos(angle).T[lane].astype(np.float32)
    sin = (np.sin(angle).T[lane] * sign[:, None]).astype(np.float32)
    tri = np.zeros((P, HALF), np.float32)
    tri[:, HALF - P:] = np.where(np.arange(P)[None, :] > np.arange(P)[:, None], -BIG, 0.0)
    sel = np.zeros((P, FB, P), np.float32)
    for m in range(FB):
        for i in range(P):
            sel[(m * P + i) // (F // NBLK), m, i] = -BIG
    eye = np.eye(P, dtype=np.float32)
    bf = mybir.dt.np(BF16)
    return {"cos": cos, "sin": sin, "ident": eye, "identb": eye.astype(bf), "tri": tri.astype(bf),
            "sel": sel.astype(bf)}


def kernel(**inputs):
    import concourse.bacc as _bacc
    from concourse.bass_utils import run_bass_kernel_spmd as _run

    a = {k: np.asarray(v) for k, v in inputs.items()}
    arrays = {
        "x": a["L0_attn_x"].reshape(B * T, D),
        "wqT": a["L0_attn_Wq"].T, "bq": a["L0_attn_bq"].reshape(KB, P).T, "wkT": a["L0_attn_Wk"].T, "bk": a["L0_attn_bk"].reshape(KB, P).T,
        "wvT": a["L0_attn_Wv"].T, "bv": a["L0_attn_bv"], "woT": a["L0_attn_Wo"].T, "bo": a["L0_attn_bo"],
        "rwT": a["L0_ffn_router_w"].T, "rb": a["L0_ffn_router_b"],
        "w1T": a["L0_ffn_w1"].T, "b1": a["L0_ffn_b1"].reshape(FB, P).T, "w2T": a["L0_ffn_w2"].T, "b2": a["L0_ffn_b2"],
    }
    arrays.update(constants())
    arrays = {f"in_{k}": np.ascontiguousarray(v) for k, v in arrays.items()}
    nc = _bacc.Bacc("TRN2", target_bir_lowering=False, num_devices=1)
    args = [nc.dram_tensor(k, v.shape, mybir.dt.from_np(v.dtype), kind="ExternalInput").ap()
            for k, v in arrays.items()]
    pieces = nc.dram_tensor("piece_scratch", [4, P, NPIECE, T], BF16, kind="Internal").ap()
    scratch = nc.dram_tensor("max_scratch", [NPIECE, GH * T], BF16, kind="Internal").ap()
    out = nc.dram_tensor("out", [B * T, D], F32, kind="ExternalOutput").ap()
    block_kernel(nc, *args, pieces, scratch, out)
    r = _run(nc, [arrays], core_ids=[0])
    return r.results[0]["out"].reshape(B, T, D)
```

```python
from contextlib import ExitStack

import numpy as np

import concourse.bass as bass
from concourse import mybir

F32 = mybir.dt.float32
BF16 = mybir.dt.bfloat16
I32 = mybir.dt.int32
ALU = mybir.AluOpType
ACT = mybir.ActivationFunctionType
AX = mybir.AxisListType

P = 128
B, T, D = 4, 1024, 256
H, HD = 16, 16
F, NBLK, TOPK = 1024, 16, 4
NT = T // P
KB = D // P
FB = F // P
GH = 4
NG = H // GH
HALF = 512
QT = T // NG
VW = 2 * HD
NTERM = 6
NPIECE = 3
KROWS = NTERM * HD
SROWS = KROWS + NPIECE
Q_PIECE = (0, 1, 2, 0, 1, 0)
K_PIECE = (0, 0, 0, 1, 1, 2)
BIG = 1e30
LOWEST = -3e38
EPS = 1e-5
SCALE = 1.0 / float(HD) ** 0.5

UNITS = [(c, j) for c in range(2) for j in range(NT) if j * P < (c + 1) * HALF]
NU = len(UNITS)
ALL_MAXU = [(i, c, min(HALF, (i + 1) * P - c * HALF)) for i in range(NT) for c in range(2) if c * HALF < (i + 1) * P]
MAXU = [ALL_MAXU[n] for n in (2, 1, 3, 7, 4, 6, 8, 10, 11, 9, 0, 5)]
NMAX = GH * len(MAXU)

S_SLOTS, M_SLOTS, P_SLOTS = 3, 3, 3
LAG = 2

PROJ = [("proj", r, c) for r in range(4) for c in range(2)]
X_TURNS = [("xnT", u) for u in range(NT // 2)]
NEXT_ROW = {0: X_TURNS[0:2], 1: X_TURNS[2:4], 2: PROJ[0:1], 3: PROJ[1:2], 4: PROJ[2:3], 5: PROJ[3:4],
            7: PROJ[4:5], 8: PROJ[5:6], 9: PROJ[6:7], 10: PROJ[7:8]}
S_FIRST = [("v", t) for t in range(NT)]
M_FIRST = X_TURNS + PROJ[0:4] + [("logits",)] + PROJ[4:8] + [("unselT",)]
S_ORDER = [("hidden", q, u) for q in range(2) for u in range(FB // 2)]
M_ORDER = [("max", 0, n) for n in range(NMAX)]
for _g in range(NG):
    M_ORDER += [("maxT", _g)]
    if _g in (0, 2):
        M_ORDER += [("ffn", 1 + _g // 2, i) for i in range(2)]
    else:
        S_ORDER += [("hidden", 2 + _g // 2, u) for u in range(FB // 2)]
    if _g:
        M_ORDER += [("oT", _g - 1, c) for c in range(2)]
    for _k in range(NU):
        S_ORDER += [("score", _g, _k, h) for h in range(GH)]
        if _g + 1 < NG:
            M_ORDER += [("max", _g + 1, n) for n in range(_k * GH, (_k + 1) * GH)]
        else:
            M_ORDER += NEXT_ROW.get(_k, [])
S_ORDER += [("v", t) for t in range(4)] + [("yT", u) for u in range(4)] + [("v", t) for t in range(4, NT)]
M_ORDER += [("ffn", 3, 0), ("oT", 3, 0), ("oT", 3, 1), ("ffn", 3, 1), ("logits",)]
M_ORDER += [("out", u) for u in range(NT // 2)] + [("unselT",)]
S_LAST = [what for what in S_ORDER if what[0] != "v"]
M_LAST = [what for what in M_ORDER if what[0] not in ("xnT", "proj", "logits", "unselT")]
N_S, N_M = len(S_ORDER), len(M_ORDER)
STACK_INC = 16 * 2 * NTERM
BASE = 1
DVE_FIRST, DVE_STEPS = 7, 31
RSQRT_MAGIC = float(0x5F3759DF)
NEWTON = 4
LN_STEPS = 2 * NT + 3 + 3 * NEWTON


def is_last(b):
    return isinstance(b, int) and b == B - 1


def s_order(b):
    return S_LAST if is_last(b) else S_ORDER


def m_order(b):
    return M_LAST if is_last(b) else M_ORDER


def s_count(b, what=None):
    n = s_order(b).index(what) + 1 if what else 0
    return b * N_S + len(S_FIRST) + n + BASE


def m_count(b, what=None):
    n = m_order(b).index(what) + 1 if what else 0
    return b * N_M + len(M_FIRST) + n + BASE


def diagonal(c, j):
    return j * P >= c * HALF


class Ring:

    def __init__(self, order, slots):
        self.order, self.slots, self.n = order, slots, 0

    def take(self, *what):
        assert self.order[self.n] == what, (self.order[self.n], what)
        self.n += 1
        return (self.n - 1) % self.slots, self.n - 1

    def end(self):
        assert self.n == len(self.order)


def block_kernel(nc, x, wqT, bq, wkT, bk, wvT, bv, woT, bo, rwT, rb, w1T, b1, w2T, b2,
                 cos_c, sin_c, ident_c, identb_c, tri_c, sel_c, piece_scratch, max_scratch, out):
    with ExitStack() as ctx:
        def sb(name, shape, dt=F32):
            return ctx.enter_context(nc.sbuf_tensor(name, shape, dt))

        def sem(name):
            return ctx.enter_context(nc.semaphore(name))

        s_bank = ctx.enter_context(nc.psum_tensor("s_bank", [P, S_SLOTS, HALF], F32))
        m_bank = ctx.enter_context(nc.psum_tensor("m_bank", [P, M_SLOTS, HALF], F32))
        o_bank = ctx.enter_context(nc.psum_tensor("o_bank", [P, 2, HALF], F32))

        x_sb = sb("x_sb", [P, NT, D])
        xnT = sb("xnT", [P, KB, T])
        yT = sb("yT", [P, KB, T])
        acc = sb("acc", [P, NT, D])
        wq_sb = sb("wq_sb", [P, KB, D])
        wk_sb = sb("wk_sb", [P, KB, D])
        wv_sb = sb("wv_sb", [P, KB, D + NBLK])
        wo_sb = sb("wo_sb", [P, KB, D])
        w1_sb = sb("w1_sb", [P, KB, F])
        w2_sb = sb("w2_sb", [P, FB, D])
        bqk_sb = sb("bqk_sb", [P, 2, KB])
        bv_sb = sb("bv_sb", [P, KB])
        rb_sb = sb("rb_sb", [P, NBLK])
        bo_sb = sb("bo_sb", [P, D])
        b2_sb = sb("b2_sb", [P, D])
        b1_sb = sb("b1_sb", [P, FB])
        cos_sb = sb("cos_sb", [P, T])
        sin_sb = sb("sin_sb", [P, T])
        ident = sb("ident", [P, P])
        identb = sb("identb", [P, P], BF16)
        tri = sb("tri", [P, HALF], BF16)
        tri_k = tri[:, HALF - P:HALF]
        sel = sb("sel", [P, FB, P], BF16)
        pieces = sb("pieces", [P, 2, NPIECE, T], BF16)
        q_st = sb("q_st", [P, 2, GH, T], BF16)
        k_st = sb("k_st", [P, 2, GH, T], BF16)
        v_sb = sb("v_sb", [P, NT, H, VW])
        probs = sb("probs", [P, P_SLOTS, GH, HALF])
        hT = sb("hT", [P, FB, QT])
        rope_sb = sb("rope_sb", [P, 2, 2, T])
        oT = sb("oT", [P, T])
        y_sb = sb("y_sb", [P, NT, D])
        unsel = sb("unsel", [P, NT, NBLK], BF16)
        unselT = sb("unselT", [P, T], BF16)
        logits = sb("logits", [P, NT, NBLK + TOPK])
        marked = sb("marked", [P, NT, NBLK + TOPK])
        top8 = sb("top8", [P, NT, 8])
        top4 = sb("top4", [P, NT, 8])
        part_max = sb("part_max", [P, 2, GH, NT, 2])
        row_max = sb("row_max", [P, GH * NT])
        max_rest = sb("max_rest", [P, GH * NT])
        max_pc = sb("max_pc", [P, NPIECE, GH * NT], BF16)
        max_pcT = sb("max_pcT", [NPIECE * GH * NT, P], BF16)
        recip = sb("recip", [P, 2, 4, GH])
        stats = sb("stats", [P, NT, 6])
        mv = sb("mv", [P, NT, 2])
        rstd = sb("rstd", [P, NT])
        var = sb("var", [P, NT])
        guess = sb("guess", [P, NT], I32)
        square = sb("square", [P, NT])

        x_in = sem("x_in")
        x_half_in = sem("x_half_in")
        acc_in = sem("acc_in")
        ident_in = sem("ident_in")
        bqk_in = sem("bqk_in")
        bias_in = sem("bias_in")
        wqk_in, wv_in, w1_in, w2_in, wo_in = (sem(n) for n in ("wqk_in", "wv_in", "w1_in", "w2_in", "wo_in"))
        mask_in = sem("mask_in")
        rope_in = sem("rope_in")
        ones_set = sem("ones_set")
        pad_set = sem("pad_set")
        ln_step = sem("ln_step")
        xn_ready = sem("xn_ready")
        acc_ready = sem("acc_ready")
        s_fill = sem("s_fill")
        s_out = sem("s_out")
        m_fill = sem("m_fill")
        m_out = sem("m_out")
        quarter_fill = sem("quarter_fill")
        quarter_out = sem("quarter_out")
        dve_step = sem("dve_step")
        turned = sem("turned")
        sin_done = sem("sin_done")
        roped = sem("roped")
        high_done = sem("high_done")
        rest_done = sem("rest_done")
        mid_done = sem("mid_done")
        low_done = sem("low_done")
        pieces_out = [sem("pieces_out0"), sem("pieces_out1")]
        stacked = [sem("stacked0"), sem("stacked1")]
        unsel_ready = sem("unsel_ready")
        max_pcs = sem("max_pcs")
        max_out = sem("max_out")
        max_left = sem("max_left")
        max_rows = sem("max_rows")
        pv_done = sem("pv_done")
        o_out = sem("o_out")
        stored = sem("stored")

        x_rows = x.rearrange("(b t p) d -> b p t d", p=P, t=NT)
        out_rows = out.rearrange("(b t p) d -> b p t d", p=P, t=NT)
        scratch_out = max_scratch.rearrange("k (r n) -> (k r) n", n=P)

        def quarter(g):
            return slice(g * QT, (g + 1) * QT)

        def rope_pair(r):
            return rope_sb[:, r % 2, 0, :], rope_sb[:, r % 2, 1, :]

        block = ctx.enter_context(nc.Block())

        @block.sync
        def _(sp):
            for count in (stored, *pieces_out, *stacked):
                sp.sem_inc(count, BASE)
            for h in range(2):
                t = slice(h * NT // 2, (h + 1) * NT // 2)
                sp.dma_start(x_sb[:, t, :], x_rows[0][:, t, :]).then_inc((x_half_in, x_in)[h], 16)
            sp.dma_start(ident[:], ident_c).then_inc(ident_in, 16)
            sp.dma_start(wq_sb[:], wqT.rearrange("(k p) n -> p k n", p=P)).then_inc(wqk_in, 16)
            sp.dma_start(wk_sb[:], wkT.rearrange("(k p) n -> p k n", p=P)).then_inc(wqk_in, 16)
            sp.dma_start(bqk_sb[:, 0, :], bq).then_inc(bqk_in, 16)
            sp.dma_start(bqk_sb[:, 1, :], bk).then_inc(bqk_in, 16)
            sp.dma_start(cos_sb[:], cos_c).then_inc(rope_in, 16)
            sp.dma_start(sin_sb[:], sin_c).then_inc(rope_in, 16)
            sp.dma_start(wv_sb[:, :, 0:D], wvT.rearrange("(k p) n -> p k n", p=P)).then_inc(wv_in, 16)
            sp.dma_start(wv_sb[:, :, D:D + NBLK], rwT.rearrange("(k p) n -> p k n", p=P)).then_inc(wv_in, 16)
            sp.dma_start(rb_sb[:], rb.partition_broadcast(P)).then_inc(bias_in, 16)
            sp.dma_start(bo_sb[:], bo.partition_broadcast(P)).then_inc(bias_in, 16)
            sp.dma_start(b2_sb[:], b2.partition_broadcast(P)).then_inc(bias_in, 16)
            sp.dma_start(b1_sb[:], b1).then_inc(bias_in, 16)
            sp.dma_start(bv_sb[:], bv).then_inc(bias_in, 16)
            sp.dma_start(identb[:], identb_c).then_inc(mask_in, 16)
            sp.dma_start(sel[:], sel_c).then_inc(mask_in, 16)
            sp.dma_start(tri[:], tri_c).then_inc(mask_in, 16)
            sp.dma_start(w1_sb[:], w1T.rearrange("(k p) n -> p k n", p=P)).then_inc(w1_in, 16)
            sp.dma_start(w2_sb[:], w2T.rearrange("(k p) n -> p k n", p=P)).then_inc(w2_in, 16)
            sp.dma_start(wo_sb[:], woT.rearrange("(k p) n -> p k n", p=P)).then_inc(wo_in, 16)

            def store_pieces(row, r):
                sp.wait_ge(low_done, row * 4 + r + 1)
                if r == 0:
                    for stack in stacked:
                        sp.nop(nofuse=True)
                        sp.wait_ge(stack, row * 2 * STACK_INC + BASE)
                sp.dma_start(piece_scratch[r], pieces[:, r % 2, :, :]).then_inc(pieces_out[r // 2], 16)

            def load_stacks(row, g, groups_done):
                mb = g // 2
                sp.wait_ge(pieces_out[mb], row * 32 + 32 + BASE)
                sp.nop(nofuse=True)
                if groups_done is not None:
                    sp.wait_ge(pv_done, groups_done * NU + BASE)
                for qk, stack, order in ((0, q_st, Q_PIECE), (1, k_st, K_PIECE)):
                    heads = piece_scratch[2 * mb + qk, (g % 2) * GH * HD:(g % 2 + 1) * GH * HD]
                    heads = heads.rearrange("(c d) k n -> k d c n", d=HD)
                    for t in range(NTERM):
                        sp.dma_start(stack[t * HD:(t + 1) * HD, g % 2, :, :],
                                     heads[order[t]]).then_inc(stacked[g % 2], 16)

            for r in range(2):
                store_pieces(0, r)
            load_stacks(0, 0, None)
            for r in range(2, 4):
                store_pieces(0, r)

            def batch_row(b):
                sp.wait_ge(stored, b * 32 + BASE)
                sp.nop(nofuse=True)
                sp.dma_start(acc[:], x_rows[b]).then_inc(acc_in, 16)
                load_stacks(b, 1, b * NG)
                if not is_last(b):
                    sp.wait_ge(m_out, m_count(b))
                    sp.nop(nofuse=True)
                    sp.dma_start(x_sb[:], x_rows[b + 1]).then_inc(x_in, 16)
                load_stacks(b, 2, b * NG + 1)
                load_stacks(b, 3, b * NG + 2)
                if not is_last(b):
                    for r in range(2):
                        store_pieces(b + 1, r)
                    load_stacks(b + 1, 0, b * NG + 3)
                    for r in range(2, 4):
                        store_pieces(b + 1, r)
                for h in range(2):
                    sp.wait_ge(m_out, m_count(b, ("out", 2 * h + 1)))
                    sp.nop(nofuse=True)
                    t = slice(h * NT // 2, (h + 1) * NT // 2)
                    sp.dma_start(out_rows[b, :, t, :], acc[:, t, :]).then_inc(stored, 16)

            with sp.Fori(0, B - 1) as b:
                batch_row(b)
            batch_row(B - 1)
            sp.wait_ge(stored, B * 32 + BASE)
            sp.wait_ge(x_in, B * 16)
            for half in range(2):
                sp.wait_ge(pieces_out[half], B * 32 + BASE)
                sp.wait_ge(stacked[half], 2 * B * STACK_INC + BASE)

        @block.gpsimd
        def _(pool):
            def rope_sin(row, r):
                pool.wait_ge(turned, row * 4 + r + 1)
                if r == 0:
                    pool.wait_ge(rope_in, 32)
                _, y2 = rope_pair(r)
                nc.gpsimd.tensor_tensor(y2, y2, sin_sb[:], ALU.mult).then_inc(sin_done, 1)

            def low_piece(row, r):
                pool.wait_ge(mid_done, row * 4 + r + 1)
                _, y2 = rope_pair(r)
                nc.gpsimd.tensor_tensor(pieces[:, r % 2, 2, :], y2, pieces[:, r % 2, 1, :],
                                        ALU.subtract).then_inc(low_done, 1)

            def rope_all(row):
                rope_sin(row, 0)
                rope_sin(row, 1)
                low_piece(row, 0)
                low_piece(row, 1)
                rope_sin(row, 2)
                rope_sin(row, 3)
                low_piece(row, 2)
                low_piece(row, 3)

            def place_maxima(b, g):
                pool.wait_ge(m_out, m_count(b, ("maxT", g)))
                pool.nop(nofuse=True)
                pool.dma_start(scratch_out, max_pcT[:]).then_inc(max_out, 16)
                pool.wait_ge(max_out, (b * NG + g + 1) * 16)
                pool.sem_inc(max_left, 1)
                pool.wait_ge(pv_done, (b * NG + max(g - 1, 0)) * NU + BASE)
                pool.nop(nofuse=True)
                pool.dma_start(q_st[KROWS:SROWS, g % 2, :, :],
                               max_scratch.rearrange("k (c n) -> k c n", c=GH)).then_inc(max_rows, 16)

            pool.sem_inc(max_left, BASE)
            nc.gpsimd.memset(unselT[:], 0.0).then_inc(ones_set, 1)
            nc.gpsimd.memset(v_sb[:, :, :, HD:VW], 1.0).then_inc(ones_set, 1)
            pool.wait_ge(ones_set, 2)
            nc.gpsimd.memset(k_st[KROWS:P, :, :, :], 1.0).then_inc(ones_set, 1)
            pool.wait_ge(ones_set, 3)
            rope_all(0)
            pool.wait_ge(low_done, 4)
            pool.wait_ge(bias_in, 16 * 5)
            nc.gpsimd.tensor_tensor(bo_sb[:], bo_sb[:], b2_sb[:], ALU.add).then_inc(ones_set, 1)

            def batch_row(b):
                pool.wait_ge(ones_set, 4)
                pool.wait_ge(acc_in, b * 16 + 16)
                nc.gpsimd.tensor_tensor(acc[:], acc[:], bo_sb[:, None, :].broadcast_to([P, NT, D]),
                                        ALU.add).then_inc(acc_ready, 1)
                for g in range(NG):
                    place_maxima(b, g)
                if not is_last(b):
                    rope_all(b + 1)

            with pool.Fori(0, B - 1) as b:
                batch_row(b)
            batch_row(B - 1)

        @block.scalar
        def _(act):
            act.sem_inc(s_out, BASE)
            act.sem_inc(o_out, BASE)

            def bank_of(ring, count, *what):
                slot, n = ring.take(*what)
                act.wait_ge(s_fill, count + n + 1)
                return s_bank[:, slot, :]

            def high_piece(row, r):
                y, _ = rope_pair(r)
                act.wait_ge(roped, row * 4 + r + 1)
                if r == 2:
                    act.wait_ge(pieces_out[0], row * 32 + 32 + BASE)
                elif r == 0:
                    act.wait_ge(pieces_out[1], row * 32 + BASE)
                nc.scalar.activation(pieces[:, r % 2, 0, :], y, ACT.Copy).then_inc(high_done, 1)

            def mid_piece(row, r):
                _, y2 = rope_pair(r)
                act.wait_ge(rest_done, row * 4 + r + 1)
                nc.scalar.activation(pieces[:, r % 2, 1, :], y2, ACT.Copy).then_inc(mid_done, 1)

            def take_v(t, bank):
                nc.scalar.activation(v_sb[:, t, :, 0:HD], bank[:, 0:D].rearrange("p (h d) -> p h d", h=H),
                                     ACT.Copy).then_inc(s_out, 1)

            first = Ring(S_FIRST, S_SLOTS)
            for r in range(2):
                high_piece(0, r)
                mid_piece(0, r)
                act.wait_ge(ones_set, 2)
                for t in range(r * NT // 2, (r + 1) * NT // 2):
                    take_v(t, bank_of(first, 0, "v", t))
            for r in range(2, 4):
                high_piece(0, r)
                mid_piece(0, r)
            first.end()

            def batch_row(b):
                ring = Ring(s_order(b), S_SLOTS)

                def filled(*what):
                    return bank_of(ring, b * N_S + len(S_FIRST), *what)

                def hidden(q):
                    if q == 1:
                        act.wait_ge(quarter_fill, b * 2 + 2)
                    elif q:
                        act.wait_ge(m_fill, m_count(b, ("ffn", q - 1, 1)))
                    for u in range(FB // 2):
                        bank = filled("hidden", q, u)
                        for i in range(2):
                            m = 2 * u + i
                            last = nc.scalar.activation(hT[:, m, :], bank[:, i * QT:(i + 1) * QT], ACT.Relu,
                                                        bias=b1_sb[:, m:m + 1])
                        last.then_inc(s_out, 1)

                def take_o(g, c):
                    act.wait_ge(pv_done, b * NG * NU + g * NU + (4 if c == 0 else NU) + BASE)
                    nc.scalar.activation(oT[:, c * HALF:(c + 1) * HALF], o_bank[:, c, :],
                                         ACT.Copy).then_inc(o_out, 1)

                def exps(g, k):
                    c, j = UNITS[k]
                    w = (c + 1) * HALF - max(c * HALF, j * P)
                    act.wait_ge(pv_done, b * NG * NU + max(g * NU + k - P_SLOTS + 1, 0) + BASE)
                    for h in range(GH):
                        nc.scalar.activation(probs[:, k % P_SLOTS, h, 0:w], filled("score", g, k, h)[:, 0:w], ACT.Exp,
                                             scale=SCALE).then_inc(s_out, 1)

                act.wait_ge(bias_in, 16 * 5)
                hidden(0)
                hidden(1)
                for g in range(NG):
                    if g in (1, 3):
                        hidden(2 + g // 2)
                    for k in range(NU):
                        exps(g, k)
                        if g == NG - 1 and k in (5, 7, 10) and not is_last(b):
                            high_piece(b + 1, (5, 7, 10).index(k))
                        if g == NG - 1 and k in (6, 8, 11) and not is_last(b):
                            mid_piece(b + 1, (6, 8, 11).index(k))
                        if k == 6:
                            take_o(g, 0)
                    take_o(g, 1)
                if not is_last(b):
                    act.wait_ge(pv_done, (b + 1) * NG * NU + BASE)
                    for t in range(4):
                        take_v(t, filled("v", t))
                    high_piece(b + 1, 3)
                for u in range(4):
                    kb, h = u // 2, u % 2
                    nc.scalar.activation(yT[:, kb, h * HALF:(h + 1) * HALF], filled("yT", u), ACT.Identity,
                                         bias=bv_sb[:, kb:kb + 1]).then_inc(s_out, 1)
                if not is_last(b):
                    for t in range(4, NT):
                        take_v(t, filled("v", t))
                    mid_piece(b + 1, 3)
                ring.end()

            with act.Fori(0, B - 1) as b:
                batch_row(b)
            batch_row(B - 1)

        @block.tensor
        def _(pe):
            pe.sem_inc(m_fill, BASE)
            pe.sem_inc(pv_done, BASE)

            def s_bank_free(ring, count, *what):
                slot, n = ring.take(*what)
                pe.wait_ge(s_out, count + max(n - S_SLOTS + 1, 0) + BASE)
                return s_bank[:, slot, :]

            def turn_x(u, bank):
                for k in range(KB):
                    for i in range(2):
                        at = (2 * k + i) * P
                        last = nc.tensor.transpose(bank[:, at:at + P], x_sb[:, 2 * u + i, k * P:(k + 1) * P], ident[:])
                last.then_inc(m_fill, 1)

            def project(r, c, k, bank):
                mb, w = r // 2, (wq_sb, wk_sb)[r % 2]
                last = nc.tensor.matmul(bank, w[:, k, mb * P:(mb + 1) * P],
                                        xnT[:, k, c * HALF:(c + 1) * HALF], start=(k == 0), stop=(k == KB - 1))
                if k == KB - 1:
                    last.then_inc(m_fill, 1)

            def route(bank):
                for t in range(NT):
                    for k in range(KB):
                        last = nc.tensor.matmul(bank[:, t * NBLK:(t + 1) * NBLK], xnT[:, k, t * P:(t + 1) * P],
                                                wv_sb[:, k, D:D + NBLK], start=(k == 0), stop=(k == KB - 1))
                last.then_inc(m_fill, 1)

            def values(t, bank):
                for k in range(KB):
                    last = nc.tensor.matmul(bank[:, 0:D], xnT[:, k, t * P:(t + 1) * P], wv_sb[:, k, 0:D],
                                            start=(k == 0), stop=(k == KB - 1))
                last.then_inc(s_fill, 1)

            def turn_unselected(row, bank):
                pe.wait_ge(unsel_ready, row + 1)
                for t in range(NT):
                    last = nc.tensor.transpose(bank.bitcast(BF16)[0:NBLK, t * P:(t + 1) * P], unsel[:, t, :], identb[:])
                last.then_inc(m_fill, 1)

            def m_bank_free(ring, count, *what):
                slot, n = ring.take(*what)
                pe.wait_ge(m_out, count + max(n - M_SLOTS + 1, 0) + BASE)
                return m_bank[:, slot, :]

            sfirst, mfirst = Ring(S_FIRST, S_SLOTS), Ring(M_FIRST, M_SLOTS)
            pe.wait_ge(ident_in, 16)
            for u in range(NT // 2):
                pe.wait_ge(xn_ready, 2 * u + 2)
                turn_x(u, m_bank_free(mfirst, 0, "xnT", u))
            pe.wait_ge(wqk_in, 32)
            pe.wait_ge(m_out, NT // 2 + BASE)
            for r in range(4):
                for c in range(2):
                    bank = m_bank_free(mfirst, 0, "proj", r, c)
                    for k in range(KB):
                        project(r, c, k, bank)
                if r == 1:
                    pe.wait_ge(wv_in, 32)
                    route(m_bank_free(mfirst, 0, "logits"))
                    for t in range(NT):
                        values(t, s_bank_free(sfirst, 0, "v", t))
            pe.wait_ge(mask_in, 48)
            turn_unselected(0, m_bank_free(mfirst, 0, "unselT"))
            pe.wait_ge(w1_in, 16)
            pe.wait_ge(w2_in, 16)
            pe.wait_ge(ones_set, 3)
            pe.wait_ge(wo_in, 16)
            sfirst.end()
            mfirst.end()

            def batch_row(b, stacks_late=False):
                sring, mring = Ring(s_order(b), S_SLOTS), Ring(m_order(b), M_SLOTS)

                def s_free(*what):
                    return s_bank_free(sring, b * N_S + len(S_FIRST), *what)

                def m_free(*what):
                    return m_bank_free(mring, b * N_M + len(M_FIRST), *what)

                def first_maxima(first, end, steps):
                    at = iter(range(steps))

                    def some():
                        n = next(at)
                        max_units(0, first + n * (end - first) // steps, first + (n + 1) * (end - first) // steps)
                    return some

                def nothing():
                    pass

                def hidden_unit(q, u, between=nothing):
                    bank = s_free("hidden", q, u)
                    for i in range(2):
                        m = 2 * u + i
                        o = bank[:, i * QT:(i + 1) * QT]
                        for k in range(KB):
                            nc.tensor.matmul(o, w1_sb[:, k, m * P:(m + 1) * P], xnT[:, k, quarter(q)],
                                             start=(k == 0), stop=False)
                            between()
                        if q == 0 and u == 0 and i == 0:
                            pe.wait_ge(m_out, m_count(b))
                        last = nc.tensor.matmul(o, sel[:, m, :], unselT[:, quarter(q)], start=False, stop=True)
                    last.then_inc(s_fill, 1)

                def ffn_tile(q, i, bank, k0=0, k1=FB, between=nothing):
                    for k in range(k0, k1):
                        if i == 0 and k % 2 == 0:
                            pe.wait_ge(s_out, s_count(b, ("hidden", q, k // 2)))
                        last = nc.tensor.matmul(bank[:, 0:D], hT[:, k, i * P:(i + 1) * P], w2_sb[:, k, :],
                                                start=(k == 0), stop=(k == FB - 1))
                        between()
                    if k1 == FB:
                        last.then_inc(quarter_fill if q == 0 else m_fill, 1)

                def max_units(g, first, end):
                    if first == 0:
                        pe.wait_ge(stacked[g % 2], (b * 2 + g // 2 + 1) * STACK_INC + BASE)
                    for n in range(first, end):
                        h, (i, c, w) = n % GH, MAXU[n // GH]
                        bank = m_free("max", g, n)
                        nc.tensor.matmul(bank[:, 0:w], q_st[0:KROWS, g % 2, h, i * P:(i + 1) * P],
                                         k_st[0:KROWS, g % 2, h, c * HALF:c * HALF + w],
                                         start=True, stop=True).then_inc(m_fill, 1)

                def turn_maxima(g, bank):
                    pe.wait_ge(max_pcs, b * NG + g + 1)
                    nc.tensor.transpose(bank.bitcast(BF16)[0:NPIECE * GH * NT, 0:P],
                                        max_pc[:].rearrange("p k r -> p (k r)"), identb[:]).then_inc(m_fill, 1)

                def turn_o(g, c):
                    pe.wait_ge(o_out, b * 2 * NG + 2 * g + c + 1 + BASE)
                    bank = m_free("oT", g, c)
                    for t in range(4):
                        last = nc.tensor.transpose(bank[:, t * P:(t + 1) * P],
                                                   oT[:, c * HALF + t * P:c * HALF + (t + 1) * P], ident[:])
                    last.then_inc(m_fill, 1)

                def scores(g, k, h):
                    c, j = UNITS[k]
                    q0 = max(c * HALF, j * P)
                    w = (c + 1) * HALF - q0
                    bank = s_free("score", g, k, h)
                    last = nc.tensor.matmul(bank[:, 0:w], k_st[0:SROWS, g % 2, h, j * P:(j + 1) * P],
                                            q_st[0:SROWS, g % 2, h, q0:q0 + w], start=True, stop=not diagonal(c, j))
                    if diagonal(c, j):
                        last = nc.tensor.matmul(bank[:, 0:P], tri_k, identb[:], start=False, stop=True)
                    last.then_inc(s_fill, 1)

                def pv(g, k):
                    c, j = UNITS[k]
                    q0 = max(c * HALF, j * P) - c * HALF
                    pe.wait_ge(s_out, s_count(b, ("score", g, k, GH - 1)))
                    if g == 0 and j == 0:
                        pe.wait_ge(quarter_out, b * 2 + 2)
                    if j == 0:
                        pe.wait_ge(o_out, b * 2 * NG + max(2 * g - 1 + c, 0) + BASE)
                    for h in range(GH):
                        last = nc.tensor.matmul(o_bank[h * VW:(h + 1) * VW, c, q0:HALF], v_sb[:, j, g * GH + h, :],
                                                probs[:, k % P_SLOTS, h, 0:HALF - q0], start=(j == 0),
                                                stop=(j == 4 * c + 3), tile_position=(0, h * VW))
                    last.then_inc(pv_done, 1)

                between = nothing if stacks_late else first_maxima(0, 16, 4 * 4)
                for u in range(4):
                    hidden_unit(0, u, between)
                between = first_maxima(0, 24, 2 * FB) if stacks_late else first_maxima(16, 32, 2 * FB)
                pe.wait_ge(o_out, b * 2 * NG + BASE)
                for i in range(2):
                    ffn_tile(0, i, o_bank[:, i, :], between=between)
                between = first_maxima(24 if stacks_late else 32, NMAX, 4 * 4)
                for u in range(4):
                    hidden_unit(1, u, between)

                for g in range(NG):
                    if g in (0, 2):
                        q = 1 + g // 2
                        turn_bank, tile0 = m_free("maxT", g), m_free("ffn", q, 0)
                        ffn_tile(q, 0, tile0, 0, 3)
                        turn_maxima(g, turn_bank)
                        ffn_tile(q, 0, tile0, 3, FB)
                        ffn_tile(q, 1, m_free("ffn", q, 1))
                    else:
                        q = 2 + g // 2
                        hidden_unit(q, 0)
                        turn_maxima(g, m_free("maxT", g))
                        for u in range(1, 4):
                            hidden_unit(q, u)
                    if g:
                        turn_o(g - 1, 0)
                        turn_o(g - 1, 1)
                    pe.wait_ge(max_rows, (b * NG + g + 1) * 16)
                    for k in range(NU):
                        work = NEXT_ROW.get(k, []) if g == NG - 1 and not is_last(b) else []
                        next_row = [(what, s) for what in work for s in range(2)]
                        for h in range(GH):
                            scores(g, k, h)
                            if g + 1 < NG:
                                max_units(g + 1, k * GH + h, k * GH + h + 1)
                            if next_row and next_row[0][0][0] == "xnT":
                                what = next_row.pop(0)[0]
                                if h % 2 == 0:
                                    pe.wait_ge(xn_ready, (b + 1) * NT + 2 * what[1] + 2)
                                    turn_x(what[1], m_free(*what))
                            elif next_row and h % 2 == 1:
                                what, s = next_row.pop(0)
                                if what == ("proj", 0, 0) and s == 0:
                                    pe.wait_ge(m_out, m_count(b, ("xnT", NT // 2 - 1)))
                                if s == 0:
                                    bank = m_free(*what)
                                project(*what[1:], s, bank)
                        if k >= LAG:
                            pv(g, k - LAG)
                    for k in range(NU - LAG, NU):
                        pv(g, k)

                ffn_tile(3, 0, m_free("ffn", 3, 0))
                turn_o(3, 0)
                turn_o(3, 1)
                ffn_tile(3, 1, m_free("ffn", 3, 1))
                if not is_last(b):
                    route(m_free("logits"))
                    for t in range(4):
                        values(t, s_free("v", t))
                pe.wait_ge(m_out, m_count(b, ("oT", 3, 1)))
                for u in range(4):
                    kb, h = u // 2, u % 2
                    bank = s_free("yT", u)
                    for t in range(4):
                        last = nc.tensor.transpose(bank[:, t * P:(t + 1) * P],
                                                   y_sb[:, 4 * h + t, kb * P:(kb + 1) * P], ident[:])
                    last.then_inc(s_fill, 1)
                if not is_last(b):
                    for t in range(4, NT):
                        values(t, s_free("v", t))
                pe.wait_ge(s_out, s_count(b, ("yT", 3)))
                for u in range(NT // 2):
                    bank = m_free("out", u)
                    for i in range(2):
                        t = 2 * u + i
                        for k in range(KB):
                            last = nc.tensor.matmul(bank[:, i * D:(i + 1) * D], yT[:, k, t * P:(t + 1) * P],
                                                    wo_sb[:, k, :], start=(k == 0), stop=(k == KB - 1))
                    last.then_inc(m_fill, 1)
                if not is_last(b):
                    turn_unselected(b + 1, m_free("unselT"))
                sring.end()
                mring.end()

            batch_row(0, stacks_late=True)
            with pe.Fori(1, B - 1) as b:
                batch_row(b)
            batch_row(B - 1)

        @block.vector
        def _(dve):
            dve.sem_inc(m_out, BASE)

            def plain():
                dve.nop(nofuse=True)

            def ln_stats(row, t):
                first = isinstance(row, int)
                if first and t == 0:
                    dve.wait_ge(x_half_in, 16)
                elif t == (NT // 2 if first else 0):
                    dve.wait_ge(x_in, row * 16 + 16)
                nc.vector.bn_stats(stats[:, t, :], x_sb[:, t, :]).then_inc(ln_step, 1)

            def ln_factors(row):
                done = row * LN_STEPS + NT
                dve.wait_ge(ln_step, done)
                plain()

                def next_step(ins):
                    nonlocal done
                    ins.then_inc(ln_step, 1)
                    done = done + 1
                    dve.wait_ge(ln_step, done)

                for t in range(NT):
                    nc.vector.bn_aggr(mv[:, t, :], stats[:, t, :]).then_inc(ln_step, 1)
                done = done + NT
                dve.wait_ge(ln_step, done)
                next_step(nc.vector.tensor_scalar(var[:], mv[:, :, 1], EPS, None, ALU.add))
                next_step(nc.vector.tensor_scalar(guess[:], var[:].bitcast(I32), 1, None, ALU.logical_shift_right))
                next_step(nc.vector.tensor_scalar(rstd[:].bitcast(I32), guess[:], -1.0, RSQRT_MAGIC,
                                                  ALU.mult, ALU.add))
                for _ in range(NEWTON):
                    next_step(nc.vector.tensor_tensor(square[:], rstd[:], rstd[:], ALU.mult))
                    next_step(nc.vector.scalar_tensor_tensor(square[:], square[:], -0.5, var[:],
                                                             ALU.mult, ALU.mult))
                    next_step(nc.vector.scalar_tensor_tensor(rstd[:], square[:], 1.5, rstd[:],
                                                             ALU.add, ALU.mult))

            def ln_apply():
                for t in range(NT):
                    nc.vector.tensor_scalar(x_sb[:, t, :], x_sb[:, t, :], mv[:, t, 0:1], rstd[:, t:t + 1],
                                            ALU.subtract, ALU.mult).then_inc(xn_ready, 1)

            def bank_of(ring, count, *what):
                slot, n = ring.take(*what)
                dve.wait_ge(m_fill, count + n + 1 + BASE)
                return m_bank[:, slot, :]

            def take_xnT(u, bank):
                t = slice(2 * u * P, 2 * (u + 1) * P)
                nc.vector.tensor_copy(xnT[:, :, t], bank.rearrange("p (k n) -> p k n", k=KB)).then_inc(m_out, 1)

            def take_projection(r, c, bank, low_count):
                mb, qk = r // 2, r % 2
                y, _ = rope_pair(r)
                if low_count is not None and c == 0:
                    dve.wait_ge(low_done, low_count)
                nc.vector.tensor_scalar(y[:, c * HALF:(c + 1) * HALF], bank, bqk_sb[:, qk, mb:mb + 1], None,
                                        ALU.add).then_inc(m_out, 1)

            def turn_halves(r, count):
                y, y2 = rope_pair(r)
                dve.wait_ge(m_out, count)
                plain()
                nc.vector.stream_shuffle(y2, y, [p ^ (HD // 2) for p in range(32)]).then_inc(turned, 1)

            def route(bank, count, link):
                nc.vector.tensor_tensor(logits[:, :, 0:NBLK],
                                        bank[:, 0:NT * NBLK].rearrange("p (t n) -> p t n", t=NT),
                                        rb_sb[:, None, :].broadcast_to([P, NT, NBLK]), ALU.add).then_inc(m_out, 1)
                dve.wait_ge(m_out, count)
                plain()
                for t in range(NT):
                    last = nc.vector.max(top8[:, t, :], logits[:, t, 0:NBLK])
                link(last)
                link(nc.vector.tensor_copy(top4[:, :, 0:TOPK], top8[:, :, 0:TOPK]))
                plain()
                for t in range(NT):
                    last = nc.vector.match_replace(marked[:, t, :], top4[:, t, :], logits[:, t, :], -LOWEST)
                link(last)
                nc.vector.tensor_tensor(unsel[:], marked[:, :, 0:NBLK], logits[:, :, 0:NBLK],
                                        ALU.is_equal).then_inc(unsel_ready, 1)

            def take_unselected(bank):
                nc.vector.tensor_copy(unselT[0:NBLK, :], bank.bitcast(BF16)[0:NBLK, :]).then_inc(m_out, 1)

            def rope_sum(row, r, link):
                y, y2 = rope_pair(r)
                if r == 0:
                    dve.wait_ge(rope_in, 32)
                dve.wait_ge(turned, row * 4 + r + 1)
                link(nc.vector.tensor_tensor(y, y, cos_sb[:], ALU.mult))
                dve.wait_ge(sin_done, row * 4 + r + 1)
                nc.vector.tensor_tensor(y, y, y2, ALU.add).then_inc(roped, 1)

            def rest(row, r):
                y, y2 = rope_pair(r)
                dve.wait_ge(high_done, row * 4 + r + 1)
                nc.vector.tensor_tensor(y2, y, pieces[:, r % 2, 0, :], ALU.subtract).then_inc(rest_done, 1)

            for t in range(NT):
                ln_stats(0, t)
            nc.vector.memset(part_max[:], LOWEST).then_inc(pad_set, 1)
            nc.vector.memset(logits[:], LOWEST).then_inc(pad_set, 1)
            nc.vector.memset(top4[:], LOWEST).then_inc(pad_set, 1)
            ln_factors(0)
            ln_apply()
            first = Ring(M_FIRST, M_SLOTS)
            first_steps = [0]

            def first_filled(*what):
                return bank_of(first, 0, *what)

            def first_link(ins):
                first_steps[0] += 1
                ins.then_inc(dve_step, 1)
                dve.wait_ge(dve_step, first_steps[0])

            def first_half(r, c):
                take_projection(r, c, first_filled("proj", r, c), r - 1 if r >= 2 else None)
                if c == 1:
                    turn_halves(r, first.n + BASE)

            for u in range(NT // 2):
                take_xnT(u, first_filled("xnT", u))
            dve.wait_ge(bqk_in, 32)
            for r in range(2):
                first_half(r, 0)
                first_half(r, 1)
            for r in range(2):
                rope_sum(0, r, first_link)
                rest(0, r)
            dve.wait_ge(bias_in, 16 * 5)
            dve.wait_ge(pad_set, 3)
            bank = first_filled("logits")
            route(bank, first.n + BASE, first_link)
            for r in range(2, 4):
                first_half(r, 0)
                first_half(r, 1)
            for r in range(2, 4):
                rope_sum(0, r, first_link)
                rest(0, r)
            bank = first_filled("unselT")
            dve.wait_ge(ones_set, 1)
            take_unselected(bank)
            first.end()
            assert first_steps[0] == DVE_FIRST, first_steps[0]

            def batch_row(b):
                ring = Ring(m_order(b), M_SLOTS)
                steps = [0]

                def filled(*what):
                    return bank_of(ring, b * N_M + len(M_FIRST), *what)

                def link(ins):
                    steps[0] += 1
                    ins.then_inc(dve_step, 1)
                    dve.wait_ge(dve_step, b * DVE_STEPS + DVE_FIRST + steps[0])

                def max_units(g, first, end):
                    for n in range(first, end):
                        h, (i, c, w) = n % GH, MAXU[n // GH]
                        bank = filled("max", g, n)
                        to = part_max[:, g % 2, h, i, c:c + 1]
                        if c * HALF + w == (i + 1) * P:
                            plain()
                            ins = nc.vector.tensor_tensor_reduce(bank[:, 0:w], bank[:, 0:w], tri[:, HALF - w:HALF],
                                                                 1.0, LOWEST, ALU.add, ALU.max, to)
                        else:
                            ins = nc.vector.tensor_reduce(to, bank[:, 0:w], AX.X, ALU.max)
                        ins.then_inc(m_out, 1)

                def split_maxima(g):
                    dve.wait_ge(m_out, m_count(b, ("max", g, NMAX - 1)))
                    link(nc.vector.tensor_reduce(row_max[:], part_max[:, g % 2].rearrange("p h i c -> p (h i) c"),
                                                 AX.X, ALU.max))
                    link(nc.vector.tensor_scalar(max_pc[:, 0, :], row_max[:], -1.0, None, ALU.mult))
                    link(nc.vector.scalar_tensor_tensor(max_rest[:], row_max[:], -1.0, max_pc[:, 0, :],
                                                        ALU.mult, ALU.subtract))
                    link(nc.vector.tensor_copy(max_pc[:, 1, :], max_rest[:]))
                    nc.vector.tensor_tensor(max_pc[:, 2, :], max_rest[:], max_pc[:, 1, :],
                                            ALU.subtract).then_inc(max_pcs, 1)

                def copy_maxima(g):
                    bank = filled("maxT", g)
                    dve.wait_ge(max_left, b * NG + g + BASE)
                    nc.vector.tensor_copy(max_pcT[:], bank.bitcast(BF16)[0:NPIECE * GH * NT, 0:P]).then_inc(m_out, 1)

                def add_ffn(q, i):
                    t = 2 * q + i
                    if q == 0:
                        dve.wait_ge(quarter_fill, b * 2 + i + 1)
                        bank, done = o_bank[:, i, :], quarter_out
                    else:
                        bank, done = filled("ffn", q, i), m_out
                    dve.wait_ge(acc_ready, b + 1)
                    nc.vector.tensor_tensor(acc[:, t, :], acc[:, t, :], bank[:, 0:D], ALU.add).then_inc(done, 1)

                def normalise(g, c):
                    bank = filled("oT", g, c).rearrange("p (t h v) -> p t h v", t=4, h=GH)
                    link(nc.vector.reciprocal(recip[:, c], bank[:, :, :, HD]))
                    o = y_sb[:, 4 * c:4 * c + 4, g * GH * HD:(g + 1) * GH * HD].rearrange("p t (h d) -> p t h d", h=GH)
                    nc.vector.tensor_tensor(o, bank[:, :, :, 0:HD],
                                            recip[:, c, :, :, None].broadcast_to([P, 4, GH, HD]),
                                            ALU.mult).then_inc(m_out, 1)

                def next_half(r, c):
                    take_projection(r, c, filled("proj", r, c), (b + 1) * 4 + r - 1)
                    if c == 1:
                        turn_halves(r, m_count(b, ("proj", r, 1)))

                max_units(0, 0, 24)
                add_ffn(0, 0)
                max_units(0, 24, 32)
                add_ffn(0, 1)
                max_units(0, 32, NMAX)
                for g in range(NG):
                    split_maxima(g)
                    copy_maxima(g)
                    if g in (0, 2):
                        add_ffn(1 + g // 2, 0)
                        add_ffn(1 + g // 2, 1)
                    if g:
                        normalise(g - 1, 0)
                        normalise(g - 1, 1)
                    for k in range(NU if g + 1 < NG else 0):
                        max_units(g + 1, k * GH, (k + 1) * GH)
                        if g == NG - 2 and not is_last(b):
                            if k < NT:
                                ln_stats(b + 1, k)
                            elif k == NT:
                                ln_factors(b + 1)
                if not is_last(b):
                    ln_apply()
                    for u in range(NT // 2):
                        take_xnT(u, filled("xnT", u))
                    next_half(0, 0)
                    next_half(0, 1)
                    next_half(1, 0)
                    rope_sum(b + 1, 0, link)
                    next_half(1, 1)
                    rest(b + 1, 0)
                    rope_sum(b + 1, 1, link)
                    next_half(2, 0)
                    rest(b + 1, 1)
                    next_half(2, 1)
                    next_half(3, 0)
                    rope_sum(b + 1, 2, link)
                    next_half(3, 1)
                    rest(b + 1, 2)
                    rope_sum(b + 1, 3, link)
                add_ffn(3, 0)
                normalise(3, 0)
                normalise(3, 1)
                add_ffn(3, 1)
                if not is_last(b):
                    bank = filled("logits")
                    route(bank, m_count(b, ("logits",)), link)
                    rest(b + 1, 3)
                dve.wait_ge(m_out, m_count(b, ("ffn", 3, 1)))
                dve.wait_ge(quarter_out, b * 2 + 2)
                for u in range(NT // 2):
                    bank = filled("out", u)
                    nc.vector.tensor_tensor(acc[:, 2 * u:2 * u + 2, :], acc[:, 2 * u:2 * u + 2, :],
                                            bank.rearrange("p (i n) -> p i n", i=2), ALU.add).then_inc(m_out, 1)
                if not is_last(b):
                    take_unselected(filled("unselT"))
                    assert steps[0] == DVE_STEPS, steps[0]
                ring.end()

            with dve.Fori(0, B - 1) as b:
                batch_row(b)
            batch_row(B - 1)


def constants():
    theta = np.power(np.float32(2500), (np.float32(-2.0) * np.arange(HD // 2, dtype=np.float32) / np.float32(HD)),
                     dtype=np.float32)
    angle = (np.arange(1, T + 1, dtype=np.float32)[:, None] * theta[None, :]).astype(np.float64)
    lane = np.arange(P) % (HD // 2)
    sign = np.where(np.arange(P) % HD < HD // 2, -1.0, 1.0)
    cos = np.cos(angle).T[lane].astype(np.float32)
    sin = (np.sin(angle).T[lane] * sign[:, None]).astype(np.float32)
    tri = np.zeros((P, HALF), np.float32)
    tri[:, HALF - P:] = np.where(np.arange(P)[None, :] > np.arange(P)[:, None], -BIG, 0.0)
    sel = np.zeros((P, FB, P), np.float32)
    for m in range(FB):
        for i in range(P):
            sel[(m * P + i) // (F // NBLK), m, i] = -BIG
    eye = np.eye(P, dtype=np.float32)
    bf = mybir.dt.np(BF16)
    return {"cos": cos, "sin": sin, "ident": eye, "identb": eye.astype(bf), "tri": tri.astype(bf),
            "sel": sel.astype(bf)}


def kernel(**inputs):
    import concourse.bacc as _bacc
    from concourse.bass_utils import run_bass_kernel_spmd as _run

    a = {k: np.asarray(v) for k, v in inputs.items()}
    arrays = {
        "x": a["L0_attn_x"].reshape(B * T, D),
        "wqT": a["L0_attn_Wq"].T, "bq": a["L0_attn_bq"].reshape(KB, P).T, "wkT": a["L0_attn_Wk"].T, "bk": a["L0_attn_bk"].reshape(KB, P).T,
        "wvT": a["L0_attn_Wv"].T, "bv": a["L0_attn_bv"].reshape(KB, P).T, "woT": a["L0_attn_Wo"].T, "bo": a["L0_attn_bo"],
        "rwT": a["L0_ffn_router_w"].T, "rb": a["L0_ffn_router_b"],
        "w1T": a["L0_ffn_w1"].T, "b1": a["L0_ffn_b1"].reshape(FB, P).T, "w2T": a["L0_ffn_w2"].T, "b2": a["L0_ffn_b2"],
    }
    arrays.update(constants())
    arrays = {f"in_{k}": np.ascontiguousarray(v) for k, v in arrays.items()}
    nc = _bacc.Bacc("TRN2", target_bir_lowering=False, num_devices=1)
    args = [nc.dram_tensor(k, v.shape, mybir.dt.from_np(v.dtype), kind="ExternalInput").ap()
            for k, v in arrays.items()]
    pieces = nc.dram_tensor("piece_scratch", [4, P, NPIECE, T], BF16, kind="Internal").ap()
    scratch = nc.dram_tensor("max_scratch", [NPIECE, GH * T], BF16, kind="Internal").ap()
    out = nc.dram_tensor("out", [B * T, D], F32, kind="ExternalOutput").ap()
    block_kernel(nc, *args, pieces, scratch, out)
    r = _run(nc, [arrays], core_ids=[0])
    return r.results[0]["out"].reshape(B, T, D)
```

```python
from contextlib import ExitStack

import numpy as np

import concourse.bass as bass
from concourse import mybir

F32 = mybir.dt.float32
BF16 = mybir.dt.bfloat16
I32 = mybir.dt.int32
ALU = mybir.AluOpType
ACT = mybir.ActivationFunctionType
AX = mybir.AxisListType

P = 128
B, T, D = 4, 1024, 256
H, HD = 16, 16
F, NBLK, TOPK = 1024, 16, 4
NT = T // P
KB = D // P
FB = F // P
GH = 4
NG = H // GH
HALF = 512
VW = 2 * HD
NTERM = 6
NPIECE = 3
KROWS = NTERM * HD
SROWS = KROWS + NPIECE
Q_PIECE = (0, 1, 2, 0, 1, 0)
K_PIECE = (0, 0, 0, 1, 1, 2)
BIG = 1e30
LOWEST = -3e38
EPS = 1e-5
SCALE = 1.0 / float(HD) ** 0.5

UNITS = [(c, j) for c in range(2) for j in range(NT) if j * P < (c + 1) * HALF]
NU = len(UNITS)
ALL_MAXU = [(i, c, min(HALF, (i + 1) * P - c * HALF)) for i in range(NT) for c in range(2) if c * HALF < (i + 1) * P]
MAXU = [ALL_MAXU[n] for n in (2, 1, 3, 7, 4, 6, 8, 10, 11, 9, 0, 5)]
NMAX = GH * len(MAXU)

S_SLOTS, M_SLOTS, P_SLOTS = 3, 3, 3
LAG = 2

PROJ = [("proj", r, c) for r in range(4) for c in range(2)]
X_TURNS = [("xnT", u) for u in range(NT // 2)]
NEXT_ROW = {0: X_TURNS[0:2], 1: X_TURNS[2:4], 2: PROJ[0:1], 3: PROJ[1:2], 4: PROJ[2:3], 5: PROJ[3:4],
            7: PROJ[4:5], 8: PROJ[5:6], 9: PROJ[6:7], 10: PROJ[7:8]}
S_FIRST = [("v", t) for t in range(NT)]
M_FIRST = X_TURNS + PROJ[0:4] + [("unselT",)] + PROJ[4:8]
HIDDEN_PARTS = {1: range(0, 4), 2: range(4, FB)}
FFN_PARTS = {0: (2, 3), 3: (4, 5)}
S_ORDER = [("hidden", 0, m) for m in range(FB)]
M_ORDER = [("max", 0, n) for n in range(NMAX)]
for _g in range(NG):
    M_ORDER += [("maxT", _g)]
    S_ORDER += [("hidden", 1, m) for m in HIDDEN_PARTS.get(_g, ())]
    M_ORDER += [("ffn", t) for t in FFN_PARTS.get(_g, ())]
    if _g:
        M_ORDER += [("oT", _g - 1, c) for c in range(2)]
    for _k in range(NU):
        S_ORDER += [("score", _g, _k, h) for h in range(GH)]
        if _g + 1 < NG:
            M_ORDER += [("max", _g + 1, n) for n in range(_k * GH, (_k + 1) * GH)]
        else:
            M_ORDER += NEXT_ROW.get(_k, [])
S_ORDER += [("v", t) for t in range(6)] + [("yT", u) for u in range(4)] + [("v", t) for t in range(6, NT)]
M_ORDER += [("ffn", 6), ("oT", 3, 0), ("oT", 3, 1), ("ffn", 7)]
M_ORDER += [("out", u) for u in range(NT // 2)] + [("unselT",)]
S_LAST = [what for what in S_ORDER if what[0] != "v"]
M_LAST = [what for what in M_ORDER if what[0] not in ("xnT", "proj", "unselT")]
N_S, N_M = len(S_ORDER), len(M_ORDER)
STACK_INC = 16 * 2 * NTERM
BASE = 1
DVE_FIRST, DVE_STEPS = 6, 32
DVE_LATE = 2
RSQRT_MAGIC = float(0x5F3759DF)
NEWTON = 4
LN_STEPS = 2 * NT + 3 + 3 * NEWTON


def is_last(b):
    return isinstance(b, int) and b == B - 1


def is_first(b):
    return isinstance(b, int) and b == 0


def s_order(b):
    return S_LAST if is_last(b) else S_ORDER


def m_order(b):
    return M_LAST if is_last(b) else M_ORDER


def s_count(b, what=None):
    n = s_order(b).index(what) + 1 if what else 0
    return b * N_S + len(S_FIRST) + n + BASE


def m_count(b, what=None):
    n = m_order(b).index(what) + 1 if what else 0
    return b * N_M + len(M_FIRST) + n + BASE


def diagonal(c, j):
    return j * P >= c * HALF


class Ring:

    def __init__(self, order, slots):
        self.order, self.slots, self.n = order, slots, 0

    def take(self, *what):
        assert self.order[self.n] == what, (self.order[self.n], what)
        self.n += 1
        return (self.n - 1) % self.slots, self.n - 1

    def end(self):
        assert self.n == len(self.order)


def block_kernel(nc, x, wqT, bq, wkT, bk, wvT, bv, woT, bo, rwT, rb, w1T, b1, w2T, b2,
                 cos_c, sin_c, ident_c, identb_c, tri_c, sel_c, piece_scratch, max_scratch, out):
    with ExitStack() as ctx:
        def sb(name, shape, dt=F32):
            return ctx.enter_context(nc.sbuf_tensor(name, shape, dt))

        def sem(name):
            return ctx.enter_context(nc.semaphore(name))

        s_bank = ctx.enter_context(nc.psum_tensor("s_bank", [P, S_SLOTS, HALF], F32))
        m_bank = ctx.enter_context(nc.psum_tensor("m_bank", [P, M_SLOTS, HALF], F32))
        o_bank = ctx.enter_context(nc.psum_tensor("o_bank", [P, 2, HALF], F32))

        x_sb = sb("x_sb", [P, NT, D])
        xnT = sb("xnT", [P, KB, T])
        yT = sb("yT", [P, KB, T])
        acc = sb("acc", [P, NT, D])
        wq_sb = sb("wq_sb", [P, KB, D])
        wk_sb = sb("wk_sb", [P, KB, D])
        wv_sb = sb("wv_sb", [P, KB, D + NBLK])
        wo_sb = sb("wo_sb", [P, KB, D])
        w1_sb = sb("w1_sb", [P, KB, F])
        w2_sb = sb("w2_sb", [P, FB, D])
        bqk_sb = sb("bqk_sb", [P, 2, KB])
        bv_sb = sb("bv_sb", [P, KB])
        rb_sb = sb("rb_sb", [P, NBLK])
        bo_sb = sb("bo_sb", [P, D])
        b2_sb = sb("b2_sb", [P, D])
        b1_sb = sb("b1_sb", [P, FB])
        cos_sb = sb("cos_sb", [P, T])
        sin_sb = sb("sin_sb", [P, T])
        ident = sb("ident", [P, P])
        identb = sb("identb", [P, P], BF16)
        tri = sb("tri", [P, HALF], BF16)
        tri_k = tri[:, HALF - P:HALF]
        sel = sb("sel", [P, FB, P], BF16)
        pieces = sb("pieces", [P, 2, NPIECE, T], BF16)
        q_st = sb("q_st", [P, 2, GH, T], BF16)
        k_st = sb("k_st", [P, 2, GH, T], BF16)
        v_sb = sb("v_sb", [P, NT, H, VW])
        probs = sb("probs", [P, P_SLOTS, GH, HALF])
        hT = sb("hT", [P, FB, HALF])
        rope_sb = sb("rope_sb", [P, 2, 2, T])
        oT = sb("oT", [P, T])
        y_sb = sb("y_sb", [P, NT, D])
        unsel = sb("unsel", [P, NT, NBLK], BF16)
        unselT = sb("unselT", [P, T], BF16)
        logits = sb("logits", [P, NT, NBLK + TOPK])
        raw_logits = sb("raw_logits", [P, NT, NBLK])
        marked = sb("marked", [P, NT, NBLK + TOPK])
        top8 = sb("top8", [P, NT, 8])
        top4 = sb("top4", [P, NT, 8])
        part_max = sb("part_max", [P, 2, GH, NT, 2])
        row_max = sb("row_max", [P, GH * NT])
        max_rest = sb("max_rest", [P, GH * NT])
        max_pc = sb("max_pc", [P, NPIECE, GH * NT], BF16)
        max_pcT = sb("max_pcT", [NPIECE * GH * NT, P], BF16)
        recip = sb("recip", [P, 2, 4, GH])
        stats = sb("stats", [P, NT, 6])
        mv = sb("mv", [P, NT, 2])
        rstd = sb("rstd", [P, NT])
        var = sb("var", [P, NT])
        guess = sb("guess", [P, NT], I32)
        square = sb("square", [P, NT])

        x_in = sem("x_in")
        x_half_in = sem("x_half_in")
        acc_in = sem("acc_in")
        ident_in = sem("ident_in")
        bqk_in = sem("bqk_in")
        bias_in = sem("bias_in")
        wqk_in, wv_in, w1_in, w2_in, wo_in = (sem(n) for n in ("wqk_in", "wv_in", "w1_in", "w2_in", "wo_in"))
        mask_in = sem("mask_in")
        rope_in = sem("rope_in")
        ones_set = sem("ones_set")
        pad_set = sem("pad_set")
        ln_step = sem("ln_step")
        xn_ready = sem("xn_ready")
        acc_ready = sem("acc_ready")
        s_fill = sem("s_fill")
        s_out = sem("s_out")
        m_fill = sem("m_fill")
        m_out = sem("m_out")
        tile_fill = sem("tile_fill")
        tile_out = sem("tile_out")
        dve_step = sem("dve_step")
        turned = sem("turned")
        sin_done = sem("sin_done")
        roped = sem("roped")
        high_done = sem("high_done")
        rest_done = sem("rest_done")
        mid_done = sem("mid_done")
        low_done = sem("low_done")
        pieces_out = [sem("pieces_out0"), sem("pieces_out1")]
        stacked = [sem("stacked0"), sem("stacked1")]
        unsel_ready = sem("unsel_ready")
        max_pcs = sem("max_pcs")
        max_out = sem("max_out")
        max_left = sem("max_left")
        max_rows = sem("max_rows")
        pv_done = sem("pv_done")
        o_out = sem("o_out")
        stored = sem("stored")

        x_rows = x.rearrange("(b t p) d -> b p t d", p=P, t=NT)
        out_rows = out.rearrange("(b t p) d -> b p t d", p=P, t=NT)
        scratch_out = max_scratch.rearrange("k (r n) -> (k r) n", n=P)

        def rope_pair(r):
            return rope_sb[:, r % 2, 0, :], rope_sb[:, r % 2, 1, :]

        block = ctx.enter_context(nc.Block())

        @block.sync
        def _(sp):
            for count in (stored, *pieces_out, *stacked):
                sp.sem_inc(count, BASE)
            for h in range(2):
                t = slice(h * NT // 2, (h + 1) * NT // 2)
                sp.dma_start(x_sb[:, t, :], x_rows[0][:, t, :]).then_inc((x_half_in, x_in)[h], 16)
            sp.dma_start(ident[:], ident_c).then_inc(ident_in, 16)
            sp.dma_start(wq_sb[:], wqT.rearrange("(k p) n -> p k n", p=P)).then_inc(wqk_in, 16)
            sp.dma_start(wk_sb[:], wkT.rearrange("(k p) n -> p k n", p=P)).then_inc(wqk_in, 16)
            sp.dma_start(bqk_sb[:, 0, :], bq).then_inc(bqk_in, 16)
            sp.dma_start(bqk_sb[:, 1, :], bk).then_inc(bqk_in, 16)
            sp.dma_start(cos_sb[:], cos_c).then_inc(rope_in, 16)
            sp.dma_start(sin_sb[:], sin_c).then_inc(rope_in, 16)
            sp.dma_start(wv_sb[:, :, 0:D], wvT.rearrange("(k p) n -> p k n", p=P)).then_inc(wv_in, 16)
            sp.dma_start(wv_sb[:, :, D:D + NBLK], rwT.rearrange("(k p) n -> p k n", p=P)).then_inc(wv_in, 16)
            sp.dma_start(rb_sb[:], rb.partition_broadcast(P)).then_inc(bias_in, 16)
            sp.dma_start(bo_sb[:], bo.partition_broadcast(P)).then_inc(bias_in, 16)
            sp.dma_start(b2_sb[:], b2.partition_broadcast(P)).then_inc(bias_in, 16)
            sp.dma_start(b1_sb[:], b1).then_inc(bias_in, 16)
            sp.dma_start(bv_sb[:], bv).then_inc(bias_in, 16)
            sp.dma_start(identb[:], identb_c).then_inc(mask_in, 16)
            sp.dma_start(sel[:], sel_c).then_inc(mask_in, 16)
            sp.dma_start(tri[:], tri_c).then_inc(mask_in, 16)
            sp.dma_start(w1_sb[:], w1T.rearrange("(k p) n -> p k n", p=P)).then_inc(w1_in, 16)
            sp.dma_start(w2_sb[:], w2T.rearrange("(k p) n -> p k n", p=P)).then_inc(w2_in, 16)
            sp.dma_start(wo_sb[:], woT.rearrange("(k p) n -> p k n", p=P)).then_inc(wo_in, 16)

            def store_pieces(row, r):
                sp.wait_ge(low_done, row * 4 + r + 1)
                if r == 0:
                    for stack in stacked:
                        sp.nop(nofuse=True)
                        sp.wait_ge(stack, row * 2 * STACK_INC + BASE)
                sp.dma_start(piece_scratch[r], pieces[:, r % 2, :, :]).then_inc(pieces_out[r // 2], 16)

            def load_stacks(row, g, groups_done):
                mb = g // 2
                sp.wait_ge(pieces_out[mb], row * 32 + 32 + BASE)
                sp.nop(nofuse=True)
                if groups_done is not None:
                    sp.wait_ge(pv_done, groups_done * NU + BASE)
                for qk, stack, order in ((0, q_st, Q_PIECE), (1, k_st, K_PIECE)):
                    heads = piece_scratch[2 * mb + qk, (g % 2) * GH * HD:(g % 2 + 1) * GH * HD]
                    heads = heads.rearrange("(c d) k n -> k d c n", d=HD)
                    for t in range(NTERM):
                        sp.dma_start(stack[t * HD:(t + 1) * HD, g % 2, :, :],
                                     heads[order[t]]).then_inc(stacked[g % 2], 16)

            for r in range(2):
                store_pieces(0, r)
            load_stacks(0, 0, None)

            def batch_row(b):
                sp.wait_ge(stored, b * 32 + BASE)
                sp.nop(nofuse=True)
                sp.dma_start(acc[:], x_rows[b]).then_inc(acc_in, 16)
                load_stacks(b, 1, b * NG)
                if not is_last(b):
                    sp.wait_ge(m_out, m_count(b))
                    sp.nop(nofuse=True)
                    sp.dma_start(x_sb[:], x_rows[b + 1]).then_inc(x_in, 16)
                if is_first(b):
                    for r in range(2, 4):
                        store_pieces(0, r)
                load_stacks(b, 2, b * NG + 1)
                load_stacks(b, 3, b * NG + 2)
                if not is_last(b):
                    for r in range(2):
                        store_pieces(b + 1, r)
                    load_stacks(b + 1, 0, b * NG + 3)
                    for r in range(2, 4):
                        store_pieces(b + 1, r)
                for h in range(2):
                    sp.wait_ge(m_out, m_count(b, ("out", 2 * h + 1)))
                    sp.nop(nofuse=True)
                    t = slice(h * NT // 2, (h + 1) * NT // 2)
                    sp.dma_start(out_rows[b, :, t, :], acc[:, t, :]).then_inc(stored, 16)

            batch_row(0)
            with sp.Fori(1, B - 1) as b:
                batch_row(b)
            batch_row(B - 1)
            sp.wait_ge(stored, B * 32 + BASE)
            sp.wait_ge(x_in, B * 16)
            for half in range(2):
                sp.wait_ge(pieces_out[half], B * 32 + BASE)
                sp.wait_ge(stacked[half], 2 * B * STACK_INC + BASE)

        @block.gpsimd
        def _(pool):
            def rope_sin(row, r):
                pool.wait_ge(turned, row * 4 + r + 1)
                if r == 0:
                    pool.wait_ge(rope_in, 32)
                _, y2 = rope_pair(r)
                nc.gpsimd.tensor_tensor(y2, y2, sin_sb[:], ALU.mult).then_inc(sin_done, 1)

            def low_piece(row, r):
                pool.wait_ge(mid_done, row * 4 + r + 1)
                _, y2 = rope_pair(r)
                nc.gpsimd.tensor_tensor(pieces[:, r % 2, 2, :], y2, pieces[:, r % 2, 1, :],
                                        ALU.subtract).then_inc(low_done, 1)

            def rope_first_heads(row):
                rope_sin(row, 0)
                rope_sin(row, 1)
                low_piece(row, 0)
                low_piece(row, 1)
                rope_sin(row, 2)
                rope_sin(row, 3)

            def place_maxima(b, g):
                pool.wait_ge(m_out, m_count(b, ("maxT", g)))
                pool.nop(nofuse=True)
                pool.dma_start(scratch_out, max_pcT[:]).then_inc(max_out, 16)
                pool.wait_ge(max_out, (b * NG + g + 1) * 16)
                pool.sem_inc(max_left, 1)
                pool.wait_ge(pv_done, (b * NG + max(g - 1, 0)) * NU + BASE)
                pool.nop(nofuse=True)
                pool.dma_start(q_st[KROWS:SROWS, g % 2, :, :],
                               max_scratch.rearrange("k (c n) -> k c n", c=GH)).then_inc(max_rows, 16)

            pool.sem_inc(max_left, BASE)
            nc.gpsimd.memset(unselT[:], 0.0).then_inc(ones_set, 1)
            nc.gpsimd.memset(v_sb[:, :, :, HD:VW], 1.0).then_inc(ones_set, 1)
            pool.wait_ge(ones_set, 2)
            nc.gpsimd.memset(k_st[KROWS:P, :, :, :], 1.0).then_inc(ones_set, 1)
            pool.wait_ge(ones_set, 3)
            rope_first_heads(0)
            pool.wait_ge(sin_done, 4)
            pool.wait_ge(bias_in, 16 * 5)
            nc.gpsimd.tensor_tensor(bo_sb[:], bo_sb[:], b2_sb[:], ALU.add).then_inc(ones_set, 1)

            def batch_row(b):
                pool.wait_ge(ones_set, 4)
                pool.wait_ge(acc_in, b * 16 + 16)
                nc.gpsimd.tensor_tensor(acc[:], acc[:], bo_sb[:, None, :].broadcast_to([P, NT, D]),
                                        ALU.add).then_inc(acc_ready, 1)
                for g in range(NG):
                    place_maxima(b, g)
                    if is_first(b) and g == 0:
                        low_piece(0, 2)
                        low_piece(0, 3)
                if not is_last(b):
                    rope_first_heads(b + 1)
                    low_piece(b + 1, 2)
                    low_piece(b + 1, 3)

            batch_row(0)
            with pool.Fori(1, B - 1) as b:
                batch_row(b)
            batch_row(B - 1)

        @block.scalar
        def _(act):
            act.sem_inc(s_out, BASE)
            act.sem_inc(o_out, BASE)

            def bank_of(ring, count, *what):
                slot, n = ring.take(*what)
                act.wait_ge(s_fill, count + n + 1)
                return s_bank[:, slot, :]

            def high_piece(row, r):
                y, _ = rope_pair(r)
                act.wait_ge(roped, row * 4 + r + 1)
                if r == 2:
                    act.wait_ge(pieces_out[0], row * 32 + 32 + BASE)
                elif r == 0:
                    act.wait_ge(pieces_out[1], row * 32 + BASE)
                nc.scalar.activation(pieces[:, r % 2, 0, :], y, ACT.Copy).then_inc(high_done, 1)

            def mid_piece(row, r):
                _, y2 = rope_pair(r)
                act.wait_ge(rest_done, row * 4 + r + 1)
                nc.scalar.activation(pieces[:, r % 2, 1, :], y2, ACT.Copy).then_inc(mid_done, 1)

            def take_v(t, bank):
                nc.scalar.activation(v_sb[:, t, :, 0:HD], bank[:, 0:D].rearrange("p (h d) -> p h d", h=H), ACT.Copy)
                nc.scalar.activation(raw_logits[:, t, :], bank[:, D:D + NBLK], ACT.Copy).then_inc(s_out, 1)

            first = Ring(S_FIRST, S_SLOTS)
            act.wait_ge(ones_set, 2)
            for t in range(NT):
                take_v(t, bank_of(first, 0, "v", t))
                if t in (NT // 2, NT // 2 + 2):
                    high_piece(0, t // 2 - NT // 4)
            mid_piece(0, 0)
            mid_piece(0, 1)
            first.end()

            def batch_row(b):
                ring = Ring(s_order(b), S_SLOTS)

                def filled(*what):
                    return bank_of(ring, b * N_S + len(S_FIRST), *what)

                def hidden(c, blocks):
                    for m in blocks:
                        nc.scalar.activation(hT[:, m, :], filled("hidden", c, m), ACT.Relu,
                                             bias=b1_sb[:, m:m + 1]).then_inc(s_out, 1)

                def take_o(g, c):
                    act.wait_ge(pv_done, b * NG * NU + g * NU + (4 if c == 0 else NU) + BASE)
                    nc.scalar.activation(oT[:, c * HALF:(c + 1) * HALF], o_bank[:, c, :],
                                         ACT.Copy).then_inc(o_out, 1)

                def exps(g, k):
                    c, j = UNITS[k]
                    w = (c + 1) * HALF - max(c * HALF, j * P)
                    act.wait_ge(pv_done, b * NG * NU + max(g * NU + k - P_SLOTS + 1, 0) + BASE)
                    for h in range(GH):
                        nc.scalar.activation(probs[:, k % P_SLOTS, h, 0:w], filled("score", g, k, h)[:, 0:w], ACT.Exp,
                                             scale=SCALE).then_inc(s_out, 1)

                act.wait_ge(bias_in, 16 * 5)
                hidden(0, range(FB))
                for g in range(NG):
                    hidden(1, HIDDEN_PARTS.get(g, ()))
                    if is_first(b) and g == 0:
                        for r in range(2, 4):
                            high_piece(0, r)
                            mid_piece(0, r)
                    for k in range(NU):
                        exps(g, k)
                        if g == NG - 1 and k in (5, 7, 10) and not is_last(b):
                            high_piece(b + 1, (5, 7, 10).index(k))
                        if g == NG - 1 and k in (6, 8, 11) and not is_last(b):
                            mid_piece(b + 1, (6, 8, 11).index(k))
                        if k == 6:
                            take_o(g, 0)
                    take_o(g, 1)
                if not is_last(b):
                    act.wait_ge(pv_done, (b + 1) * NG * NU + BASE)
                    for t in range(6):
                        take_v(t, filled("v", t))
                for u in range(4):
                    kb, h = u // 2, u % 2
                    nc.scalar.activation(yT[:, kb, h * HALF:(h + 1) * HALF], filled("yT", u), ACT.Identity,
                                         bias=bv_sb[:, kb:kb + 1]).then_inc(s_out, 1)
                if not is_last(b):
                    for t in range(6, NT):
                        take_v(t, filled("v", t))
                    high_piece(b + 1, 3)
                    mid_piece(b + 1, 3)
                ring.end()

            batch_row(0)
            with act.Fori(1, B - 1) as b:
                batch_row(b)
            batch_row(B - 1)

        @block.tensor
        def _(pe):
            pe.sem_inc(m_fill, BASE)
            pe.sem_inc(pv_done, BASE)

            def s_bank_free(ring, count, *what):
                slot, n = ring.take(*what)
                pe.wait_ge(s_out, count + max(n - S_SLOTS + 1, 0) + BASE)
                return s_bank[:, slot, :]

            def turn_x(u, bank):
                for k in range(KB):
                    for i in range(2):
                        at = (2 * k + i) * P
                        last = nc.tensor.transpose(bank[:, at:at + P], x_sb[:, 2 * u + i, k * P:(k + 1) * P], ident[:])
                last.then_inc(m_fill, 1)

            def project(r, c, k, bank):
                mb, w = r // 2, (wq_sb, wk_sb)[r % 2]
                last = nc.tensor.matmul(bank, w[:, k, mb * P:(mb + 1) * P],
                                        xnT[:, k, c * HALF:(c + 1) * HALF], start=(k == 0), stop=(k == KB - 1))
                if k == KB - 1:
                    last.then_inc(m_fill, 1)

            def values(t, bank):
                for k in range(KB):
                    last = nc.tensor.matmul(bank[:, 0:D + NBLK], xnT[:, k, t * P:(t + 1) * P], wv_sb[:, k, :],
                                            start=(k == 0), stop=(k == KB - 1))
                last.then_inc(s_fill, 1)

            def turn_unselected(row, bank):
                pe.wait_ge(unsel_ready, row + 1)
                for t in range(NT):
                    last = nc.tensor.transpose(bank.bitcast(BF16)[0:NBLK, t * P:(t + 1) * P], unsel[:, t, :], identb[:])
                last.then_inc(m_fill, 1)

            def m_bank_free(ring, count, *what):
                slot, n = ring.take(*what)
                pe.wait_ge(m_out, count + max(n - M_SLOTS + 1, 0) + BASE)
                return m_bank[:, slot, :]

            sfirst, mfirst = Ring(S_FIRST, S_SLOTS), Ring(M_FIRST, M_SLOTS)
            pe.wait_ge(ident_in, 16)
            for u in range(NT // 2):
                pe.wait_ge(xn_ready, 2 * u + 2)
                turn_x(u, m_bank_free(mfirst, 0, "xnT", u))
            pe.wait_ge(wqk_in, 32)
            pe.wait_ge(m_out, NT // 2 + BASE)
            for r in range(4):
                for c in range(2):
                    bank = m_bank_free(mfirst, 0, "proj", r, c)
                    for k in range(KB):
                        project(r, c, k, bank)
                if r == 1:
                    pe.wait_ge(wv_in, 32)
                    for t in range(NT):
                        values(t, s_bank_free(sfirst, 0, "v", t))
                    pe.wait_ge(mask_in, 48)
                    turn_unselected(0, m_bank_free(mfirst, 0, "unselT"))
            pe.wait_ge(w1_in, 16)
            pe.wait_ge(w2_in, 16)
            pe.wait_ge(ones_set, 3)
            pe.wait_ge(wo_in, 16)
            sfirst.end()
            mfirst.end()

            def batch_row(b):
                stacks_late = is_first(b)
                sring, mring = Ring(s_order(b), S_SLOTS), Ring(m_order(b), M_SLOTS)

                def s_free(*what):
                    return s_bank_free(sring, b * N_S + len(S_FIRST), *what)

                def m_free(*what):
                    return m_bank_free(mring, b * N_M + len(M_FIRST), *what)

                def first_maxima(first, end, steps):
                    at = iter(range(steps))

                    def some():
                        n = next(at)
                        max_units(0, first + n * (end - first) // steps, first + (n + 1) * (end - first) // steps)
                    return some

                def nothing():
                    pass

                def hidden_unit(c, m, between=nothing):
                    bank = s_free("hidden", c, m)
                    tokens = slice(c * HALF, (c + 1) * HALF)
                    for k in range(KB):
                        nc.tensor.matmul(bank, w1_sb[:, k, m * P:(m + 1) * P], xnT[:, k, tokens],
                                         start=(k == 0), stop=False)
                        between()
                    if c == 0 and m == 0:
                        pe.wait_ge(m_out, m_count(b))
                    nc.tensor.matmul(bank, sel[:, m, :], unselT[:, tokens], start=False, stop=True).then_inc(s_fill, 1)

                def ffn_tile(t, bank, between=nothing):
                    for k in range(FB):
                        if t == 0 or (t == 4 and k == 0):
                            pe.wait_ge(s_out, s_count(b, ("hidden", 0, k) if t == 0 else ("hidden", 1, FB - 1)))
                        last = nc.tensor.matmul(bank[:, 0:D], hT[:, k, t % 4 * P:(t % 4 + 1) * P], w2_sb[:, k, :],
                                                start=(k == 0), stop=(k == FB - 1))
                        between()
                    last.then_inc(tile_fill if t < 2 else m_fill, 1)

                def max_units(g, first, end):
                    if first == 0:
                        pe.wait_ge(stacked[g % 2], (b * 2 + g // 2 + 1) * STACK_INC + BASE)
                    for n in range(first, end):
                        h, (i, c, w) = n % GH, MAXU[n // GH]
                        bank = m_free("max", g, n)
                        nc.tensor.matmul(bank[:, 0:w], q_st[0:KROWS, g % 2, h, i * P:(i + 1) * P],
                                         k_st[0:KROWS, g % 2, h, c * HALF:c * HALF + w],
                                         start=True, stop=True).then_inc(m_fill, 1)

                def turn_maxima(g, bank):
                    pe.wait_ge(max_pcs, b * NG + g + 1)
                    nc.tensor.transpose(bank.bitcast(BF16)[0:NPIECE * GH * NT, 0:P],
                                        max_pc[:].rearrange("p k r -> p (k r)"), identb[:]).then_inc(m_fill, 1)

                def turn_o(g, c):
                    pe.wait_ge(o_out, b * 2 * NG + 2 * g + c + 1 + BASE)
                    bank = m_free("oT", g, c)
                    for t in range(4):
                        last = nc.tensor.transpose(bank[:, t * P:(t + 1) * P],
                                                   oT[:, c * HALF + t * P:c * HALF + (t + 1) * P], ident[:])
                    last.then_inc(m_fill, 1)

                def scores(g, k, h):
                    c, j = UNITS[k]
                    q0 = max(c * HALF, j * P)
                    w = (c + 1) * HALF - q0
                    bank = s_free("score", g, k, h)
                    last = nc.tensor.matmul(bank[:, 0:w], k_st[0:SROWS, g % 2, h, j * P:(j + 1) * P],
                                            q_st[0:SROWS, g % 2, h, q0:q0 + w], start=True, stop=not diagonal(c, j))
                    if diagonal(c, j):
                        last = nc.tensor.matmul(bank[:, 0:P], tri_k, identb[:], start=False, stop=True)
                    last.then_inc(s_fill, 1)

                def pv(g, k):
                    c, j = UNITS[k]
                    q0 = max(c * HALF, j * P) - c * HALF
                    pe.wait_ge(s_out, s_count(b, ("score", g, k, GH - 1)))
                    if g == 0 and j == 0:
                        pe.wait_ge(tile_out, b * 2 + 2)
                    if j == 0:
                        pe.wait_ge(o_out, b * 2 * NG + max(2 * g - 1 + c, 0) + BASE)
                    for h in range(GH):
                        last = nc.tensor.matmul(o_bank[h * VW:(h + 1) * VW, c, q0:HALF], v_sb[:, j, g * GH + h, :],
                                                probs[:, k % P_SLOTS, h, 0:HALF - q0], start=(j == 0),
                                                stop=(j == 4 * c + 3), tile_position=(0, h * VW))
                    last.then_inc(pv_done, 1)

                if stacks_late:
                    for m in range(4):
                        hidden_unit(0, m)
                hidden_max = 16 if stacks_late else 32
                some = first_maxima(0, hidden_max, 8 if stacks_late else 16)
                for m in range(4 if stacks_late else 0, FB):
                    hidden_unit(0, m, some)
                pe.wait_ge(o_out, b * 2 * NG + BASE)
                some = first_maxima(hidden_max, NMAX, 2 * FB)
                for t in range(2):
                    ffn_tile(t, o_bank[:, t, :], some)

                for g in range(NG):
                    turn_bank = m_free("maxT", g)
                    turn_after = iter(range(100))

                    def turn():
                        if next(turn_after) == (0 if g in HIDDEN_PARTS else 2):
                            turn_maxima(g, turn_bank)

                    for m in HIDDEN_PARTS.get(g, ()):
                        hidden_unit(1, m, turn)
                    for t in FFN_PARTS.get(g, ()):
                        ffn_tile(t, m_free("ffn", t), turn)
                    if g:
                        turn_o(g - 1, 0)
                        turn_o(g - 1, 1)
                    pe.wait_ge(max_rows, (b * NG + g + 1) * 16)
                    for k in range(NU):
                        work = NEXT_ROW.get(k, []) if g == NG - 1 and not is_last(b) else []
                        next_row = [(what, s) for what in work for s in range(2)]
                        for h in range(GH):
                            scores(g, k, h)
                            if g + 1 < NG:
                                max_units(g + 1, k * GH + h, k * GH + h + 1)
                            if next_row and next_row[0][0][0] == "xnT":
                                what = next_row.pop(0)[0]
                                if h % 2 == 0:
                                    pe.wait_ge(xn_ready, (b + 1) * NT + 2 * what[1] + 2)
                                    turn_x(what[1], m_free(*what))
                            elif next_row and h % 2 == 1:
                                what, s = next_row.pop(0)
                                if what == ("proj", 0, 0) and s == 0:
                                    pe.wait_ge(m_out, m_count(b, ("xnT", NT // 2 - 1)))
                                if s == 0:
                                    bank = m_free(*what)
                                project(*what[1:], s, bank)
                        if k >= LAG:
                            pv(g, k - LAG)
                    for k in range(NU - LAG, NU):
                        pv(g, k)

                ffn_tile(6, m_free("ffn", 6))
                turn_o(3, 0)
                turn_o(3, 1)
                ffn_tile(7, m_free("ffn", 7))
                if not is_last(b):
                    for t in range(6):
                        values(t, s_free("v", t))
                pe.wait_ge(m_out, m_count(b, ("oT", 3, 1)))
                for u in range(4):
                    kb, h = u // 2, u % 2
                    bank = s_free("yT", u)
                    for t in range(4):
                        last = nc.tensor.transpose(bank[:, t * P:(t + 1) * P],
                                                   y_sb[:, 4 * h + t, kb * P:(kb + 1) * P], ident[:])
                    last.then_inc(s_fill, 1)
                if not is_last(b):
                    for t in range(6, NT):
                        values(t, s_free("v", t))
                pe.wait_ge(s_out, s_count(b, ("yT", 3)))
                for u in range(NT // 2):
                    bank = m_free("out", u)
                    for i in range(2):
                        t = 2 * u + i
                        for k in range(KB):
                            last = nc.tensor.matmul(bank[:, i * D:(i + 1) * D], yT[:, k, t * P:(t + 1) * P],
                                                    wo_sb[:, k, :], start=(k == 0), stop=(k == KB - 1))
                    last.then_inc(m_fill, 1)
                if not is_last(b):
                    turn_unselected(b + 1, m_free("unselT"))
                sring.end()
                mring.end()

            batch_row(0)
            with pe.Fori(1, B - 1) as b:
                batch_row(b)
            batch_row(B - 1)

        @block.vector
        def _(dve):
            dve.sem_inc(m_out, BASE)

            def plain():
                dve.nop(nofuse=True)

            def ln_stats(row, t):
                first = isinstance(row, int)
                if first and t == 0:
                    dve.wait_ge(x_half_in, 16)
                elif t == (NT // 2 if first else 0):
                    dve.wait_ge(x_in, row * 16 + 16)
                nc.vector.bn_stats(stats[:, t, :], x_sb[:, t, :]).then_inc(ln_step, 1)

            def ln_factors(row):
                done = row * LN_STEPS + NT
                dve.wait_ge(ln_step, done)
                plain()

                def next_step(ins):
                    nonlocal done
                    ins.then_inc(ln_step, 1)
                    done = done + 1
                    dve.wait_ge(ln_step, done)

                for t in range(NT):
                    nc.vector.bn_aggr(mv[:, t, :], stats[:, t, :]).then_inc(ln_step, 1)
                done = done + NT
                dve.wait_ge(ln_step, done)
                next_step(nc.vector.tensor_scalar(var[:], mv[:, :, 1], EPS, None, ALU.add))
                next_step(nc.vector.tensor_scalar(guess[:], var[:].bitcast(I32), 1, None, ALU.logical_shift_right))
                next_step(nc.vector.tensor_scalar(rstd[:].bitcast(I32), guess[:], -1.0, RSQRT_MAGIC,
                                                  ALU.mult, ALU.add))
                for _ in range(NEWTON):
                    next_step(nc.vector.tensor_tensor(square[:], rstd[:], rstd[:], ALU.mult))
                    next_step(nc.vector.scalar_tensor_tensor(square[:], square[:], -0.5, var[:],
                                                             ALU.mult, ALU.mult))
                    next_step(nc.vector.scalar_tensor_tensor(rstd[:], square[:], 1.5, rstd[:],
                                                             ALU.add, ALU.mult))

            def ln_apply():
                for t in range(NT):
                    nc.vector.tensor_scalar(x_sb[:, t, :], x_sb[:, t, :], mv[:, t, 0:1], rstd[:, t:t + 1],
                                            ALU.subtract, ALU.mult).then_inc(xn_ready, 1)

            def bank_of(ring, count, *what):
                slot, n = ring.take(*what)
                dve.wait_ge(m_fill, count + n + 1 + BASE)
                return m_bank[:, slot, :]

            def take_xnT(u, bank):
                t = slice(2 * u * P, 2 * (u + 1) * P)
                nc.vector.tensor_copy(xnT[:, :, t], bank.rearrange("p (k n) -> p k n", k=KB)).then_inc(m_out, 1)

            def take_projection(r, c, bank, low_count):
                mb, qk = r // 2, r % 2
                y, _ = rope_pair(r)
                if low_count is not None and c == 0:
                    dve.wait_ge(low_done, low_count)
                nc.vector.tensor_scalar(y[:, c * HALF:(c + 1) * HALF], bank, bqk_sb[:, qk, mb:mb + 1], None,
                                        ALU.add).then_inc(m_out, 1)

            def turn_halves(r, count):
                y, y2 = rope_pair(r)
                dve.wait_ge(m_out, count)
                plain()
                nc.vector.stream_shuffle(y2, y, [p ^ (HD // 2) for p in range(32)]).then_inc(turned, 1)

            def route(count, link):
                dve.wait_ge(s_out, count)
                link(nc.vector.tensor_tensor(logits[:, :, 0:NBLK], raw_logits[:],
                                             rb_sb[:, None, :].broadcast_to([P, NT, NBLK]), ALU.add))
                plain()
                for t in range(NT):
                    last = nc.vector.max(top8[:, t, :], logits[:, t, 0:NBLK])
                link(last)
                link(nc.vector.tensor_copy(top4[:, :, 0:TOPK], top8[:, :, 0:TOPK]))
                plain()
                for t in range(NT):
                    last = nc.vector.match_replace(marked[:, t, :], top4[:, t, :], logits[:, t, :], -LOWEST)
                link(last)
                nc.vector.tensor_tensor(unsel[:], marked[:, :, 0:NBLK], logits[:, :, 0:NBLK],
                                        ALU.is_equal).then_inc(unsel_ready, 1)

            def take_unselected(bank):
                nc.vector.tensor_copy(unselT[0:NBLK, :], bank.bitcast(BF16)[0:NBLK, :]).then_inc(m_out, 1)

            def rope_sum(row, r, link):
                y, y2 = rope_pair(r)
                if r == 0:
                    dve.wait_ge(rope_in, 32)
                dve.wait_ge(turned, row * 4 + r + 1)
                link(nc.vector.tensor_tensor(y, y, cos_sb[:], ALU.mult))
                dve.wait_ge(sin_done, row * 4 + r + 1)
                nc.vector.tensor_tensor(y, y, y2, ALU.add).then_inc(roped, 1)

            def rest(row, r):
                y, y2 = rope_pair(r)
                dve.wait_ge(high_done, row * 4 + r + 1)
                nc.vector.tensor_tensor(y2, y, pieces[:, r % 2, 0, :], ALU.subtract).then_inc(rest_done, 1)

            for t in range(NT):
                ln_stats(0, t)
            nc.vector.memset(part_max[:], LOWEST).then_inc(pad_set, 1)
            nc.vector.memset(logits[:], LOWEST).then_inc(pad_set, 1)
            nc.vector.memset(top4[:], LOWEST).then_inc(pad_set, 1)
            ln_factors(0)
            ln_apply()
            first = Ring(M_FIRST, M_SLOTS)
            first_steps = [0]

            def first_filled(*what):
                return bank_of(first, 0, *what)

            def first_link(ins):
                first_steps[0] += 1
                ins.then_inc(dve_step, 1)
                dve.wait_ge(dve_step, first_steps[0])

            def first_half(r, c):
                take_projection(r, c, first_filled("proj", r, c), r - 1 if r >= 2 else None)
                if c == 1:
                    turn_halves(r, first.n + BASE)

            for u in range(NT // 2):
                take_xnT(u, first_filled("xnT", u))
            dve.wait_ge(bqk_in, 32)
            for r in range(2):
                first_half(r, 0)
                first_half(r, 1)
            rope_sum(0, 0, first_link)
            rope_sum(0, 1, first_link)
            rest(0, 0)
            rest(0, 1)
            dve.wait_ge(bias_in, 16 * 5)
            dve.wait_ge(pad_set, 3)
            route(NT + BASE, first_link)
            bank = first_filled("unselT")
            dve.wait_ge(ones_set, 1)
            take_unselected(bank)
            for r in range(2, 4):
                first_half(r, 0)
                first_half(r, 1)
            first.end()
            assert first_steps[0] == DVE_FIRST, first_steps[0]

            def batch_row(b):
                ring = Ring(m_order(b), M_SLOTS)
                steps = [0]

                def filled(*what):
                    return bank_of(ring, b * N_M + len(M_FIRST), *what)

                def link(ins):
                    steps[0] += 1
                    ins.then_inc(dve_step, 1)
                    before = DVE_FIRST if is_first(b) else b * DVE_STEPS + DVE_FIRST + DVE_LATE
                    dve.wait_ge(dve_step, before + steps[0])

                def max_units(g, first, end):
                    for n in range(first, end):
                        h, (i, c, w) = n % GH, MAXU[n // GH]
                        bank = filled("max", g, n)
                        to = part_max[:, g % 2, h, i, c:c + 1]
                        if c * HALF + w == (i + 1) * P:
                            plain()
                            ins = nc.vector.tensor_tensor_reduce(bank[:, 0:w], bank[:, 0:w], tri[:, HALF - w:HALF],
                                                                 1.0, LOWEST, ALU.add, ALU.max, to)
                        else:
                            ins = nc.vector.tensor_reduce(to, bank[:, 0:w], AX.X, ALU.max)
                        ins.then_inc(m_out, 1)

                def split_maxima(g):
                    dve.wait_ge(m_out, m_count(b, ("max", g, NMAX - 1)))
                    link(nc.vector.tensor_reduce(row_max[:], part_max[:, g % 2].rearrange("p h i c -> p (h i) c"),
                                                 AX.X, ALU.max))
                    link(nc.vector.tensor_scalar(max_pc[:, 0, :], row_max[:], -1.0, None, ALU.mult))
                    link(nc.vector.scalar_tensor_tensor(max_rest[:], row_max[:], -1.0, max_pc[:, 0, :],
                                                        ALU.mult, ALU.subtract))
                    link(nc.vector.tensor_copy(max_pc[:, 1, :], max_rest[:]))
                    nc.vector.tensor_tensor(max_pc[:, 2, :], max_rest[:], max_pc[:, 1, :],
                                            ALU.subtract).then_inc(max_pcs, 1)

                def copy_maxima(g):
                    bank = filled("maxT", g)
                    dve.wait_ge(max_left, b * NG + g + BASE)
                    nc.vector.tensor_copy(max_pcT[:], bank.bitcast(BF16)[0:NPIECE * GH * NT, 0:P]).then_inc(m_out, 1)

                def add_ffn(t):
                    if t < 2:
                        dve.wait_ge(tile_fill, b * 2 + t + 1)
                        bank, done = o_bank[:, t, :], tile_out
                    else:
                        bank, done = filled("ffn", t), m_out
                    dve.wait_ge(acc_ready, b + 1)
                    nc.vector.tensor_tensor(acc[:, t, :], acc[:, t, :], bank[:, 0:D], ALU.add).then_inc(done, 1)

                def normalise(g, c):
                    bank = filled("oT", g, c).rearrange("p (t h v) -> p t h v", t=4, h=GH)
                    link(nc.vector.reciprocal(recip[:, c], bank[:, :, :, HD]))
                    o = y_sb[:, 4 * c:4 * c + 4, g * GH * HD:(g + 1) * GH * HD].rearrange("p t (h d) -> p t h d", h=GH)
                    nc.vector.tensor_tensor(o, bank[:, :, :, 0:HD],
                                            recip[:, c, :, :, None].broadcast_to([P, 4, GH, HD]),
                                            ALU.mult).then_inc(m_out, 1)

                def next_half(r, c):
                    take_projection(r, c, filled("proj", r, c), (b + 1) * 4 + r - 1)
                    if c == 1:
                        turn_halves(r, m_count(b, ("proj", r, 1)))

                max_units(0, 0, 40)
                add_ffn(0)
                max_units(0, 40, NMAX)
                add_ffn(1)
                for g in range(NG):
                    split_maxima(g)
                    copy_maxima(g)
                    if g == 0 and is_first(b):
                        for r in range(2, 4):
                            rope_sum(0, r, link)
                            rest(0, r)
                    if g == NG - 2 and not is_last(b):
                        for t in range(NT):
                            ln_stats(b + 1, t)
                        ln_factors(b + 1)
                    if g == NG - 1 and not is_last(b):
                        ln_apply()
                    for t in FFN_PARTS.get(g, ()):
                        add_ffn(t)
                    if g:
                        normalise(g - 1, 0)
                        normalise(g - 1, 1)
                    if g + 1 < NG:
                        max_units(g + 1, 0, NMAX)
                if not is_last(b):
                    for u in range(NT // 2):
                        take_xnT(u, filled("xnT", u))
                    next_half(0, 0)
                    next_half(0, 1)
                    next_half(1, 0)
                    rope_sum(b + 1, 0, link)
                    next_half(1, 1)
                    rest(b + 1, 0)
                    rope_sum(b + 1, 1, link)
                    next_half(2, 0)
                    rest(b + 1, 1)
                    next_half(2, 1)
                    next_half(3, 0)
                    rope_sum(b + 1, 2, link)
                    next_half(3, 1)
                    rest(b + 1, 2)
                    rope_sum(b + 1, 3, link)
                add_ffn(6)
                normalise(3, 0)
                normalise(3, 1)
                add_ffn(7)
                if not is_last(b):
                    route(s_count(b, ("v", NT - 1)), link)
                dve.wait_ge(m_out, m_count(b, ("ffn", 7)))
                dve.wait_ge(tile_out, b * 2 + 2)
                for u in range(NT // 2):
                    bank = filled("out", u)
                    nc.vector.tensor_tensor(acc[:, 2 * u:2 * u + 2, :], acc[:, 2 * u:2 * u + 2, :],
                                            bank.rearrange("p (i n) -> p i n", i=2), ALU.add).then_inc(m_out, 1)
                if not is_last(b):
                    rest(b + 1, 3)
                    take_unselected(filled("unselT"))
                    assert steps[0] == DVE_STEPS + DVE_LATE * is_first(b), steps[0]
                ring.end()

            batch_row(0)
            with dve.Fori(1, B - 1) as b:
                batch_row(b)
            batch_row(B - 1)


def constants():
    theta = np.power(np.float32(2500), (np.float32(-2.0) * np.arange(HD // 2, dtype=np.float32) / np.float32(HD)),
                     dtype=np.float32)
    angle = (np.arange(1, T + 1, dtype=np.float32)[:, None] * theta[None, :]).astype(np.float64)
    lane = np.arange(P) % (HD // 2)
    sign = np.where(np.arange(P) % HD < HD // 2, -1.0, 1.0)
    cos = np.cos(angle).T[lane].astype(np.float32)
    sin = (np.sin(angle).T[lane] * sign[:, None]).astype(np.float32)
    tri = np.zeros((P, HALF), np.float32)
    tri[:, HALF - P:] = np.where(np.arange(P)[None, :] > np.arange(P)[:, None], -BIG, 0.0)
    sel = np.zeros((P, FB, P), np.float32)
    for m in range(FB):
        for i in range(P):
            sel[(m * P + i) // (F // NBLK), m, i] = -BIG
    eye = np.eye(P, dtype=np.float32)
    bf = mybir.dt.np(BF16)
    return {"cos": cos, "sin": sin, "ident": eye, "identb": eye.astype(bf), "tri": tri.astype(bf),
            "sel": sel.astype(bf)}


def kernel(**inputs):
    import concourse.bacc as _bacc
    from concourse.bass_utils import run_bass_kernel_spmd as _run

    a = {k: np.asarray(v) for k, v in inputs.items()}
    arrays = {
        "x": a["L0_attn_x"].reshape(B * T, D),
        "wqT": a["L0_attn_Wq"].T, "bq": a["L0_attn_bq"].reshape(KB, P).T, "wkT": a["L0_attn_Wk"].T, "bk": a["L0_attn_bk"].reshape(KB, P).T,
        "wvT": a["L0_attn_Wv"].T, "bv": a["L0_attn_bv"].reshape(KB, P).T, "woT": a["L0_attn_Wo"].T, "bo": a["L0_attn_bo"],
        "rwT": a["L0_ffn_router_w"].T, "rb": a["L0_ffn_router_b"],
        "w1T": a["L0_ffn_w1"].T, "b1": a["L0_ffn_b1"].reshape(FB, P).T, "w2T": a["L0_ffn_w2"].T, "b2": a["L0_ffn_b2"],
    }
    arrays.update(constants())
    arrays = {f"in_{k}": np.ascontiguousarray(v) for k, v in arrays.items()}
    nc = _bacc.Bacc("TRN2", target_bir_lowering=False, num_devices=1)
    args = [nc.dram_tensor(k, v.shape, mybir.dt.from_np(v.dtype), kind="ExternalInput").ap()
            for k, v in arrays.items()]
    pieces = nc.dram_tensor("piece_scratch", [4, P, NPIECE, T], BF16, kind="Internal").ap()
    scratch = nc.dram_tensor("max_scratch", [NPIECE, GH * T], BF16, kind="Internal").ap()
    out = nc.dram_tensor("out", [B * T, D], F32, kind="ExternalOutput").ap()
    block_kernel(nc, *args, pieces, scratch, out)
    r = _run(nc, [arrays], core_ids=[0])
    return r.results[0]["out"].reshape(B, T, D)
```
